# Optimizing a Trainium2 kernel written in Bass

```python
import numpy as np
import jax
import jax.numpy as jnp

def _softmax(x, axis=-1):
    return jax.nn.softmax(x, axis=axis)

def _gelu(x):
    return jax.nn.gelu(x, approximate=True)

def _silu(x):
    return jax.nn.silu(x)

def _sigmoid(x):
    return jax.nn.sigmoid(x)

def _layernorm(x, axis=-1, eps=1e-05):
    m = jnp.mean(x, axis=axis, keepdims=True)
    v = jnp.var(x, axis=axis, keepdims=True)
    return (x - m) / jnp.sqrt(v + eps)

def _scatter_add(tgt, idx, src, axis=0):
    return tgt.at[idx].add(src)

def _segment_sum(src, seg, n):
    return jax.ops.segment_sum(src, seg, n)
kernel_name = 'mk_cond_resid_d2_seqx_r8_403dd4'

def setup_inputs(seed: int=0):
    np.random.seed(seed)
    _w = jnp.asarray

    def _rec_inputs():
        import jax
        import jax.numpy as jnp
        _rk = jax.random.key(seed)
        x = -0.000125 + 0.9999 * jax.random.normal(jax.random.fold_in(_rk, 1), (8, 128, 512), jnp.float32)
        _lenS = 128 - jax.random.randint(jax.random.fold_in(_rk, 7), (8,), 0, max(1, 128 // 4) + 1, jnp.int32)
        _lenS2 = 128 - jax.random.randint(jax.random.fold_in(_rk, 8), (8,), 0, max(1, 128 // 4) + 1, jnp.int32)
        itok_B_0_23 = jax.random.randint(jax.random.fold_in(_rk, 11), (8,), 0, 24, jnp.int32)
        itok_B_2_6 = jax.random.randint(jax.random.fold_in(_rk, 12), (8,), 2, 7, jnp.int32)
        return (x, itok_B_0_23, itok_B_2_6)
    x, itok_B_0_23, itok_B_2_6 = _rec_inputs()

    def _L0_cond_setup():
        import jax, jax.numpy as jnp
        import numpy as np
        R = 16
        ALPHA = 32
        SCALING = ALPHA / R
        SLOTS = 32
        IN_F = 512
        OUT_F = 512
        B, T = (8, 128)
        key = jax.random.key(seed)
        k1, k2, k3, k4, k5, k6 = jax.random.split(key, 6)
        x = jax.random.normal(k1, (B, T, IN_F), dtype=jnp.float32)
        adapter_mapping = jax.random.randint(k2, (B,), 0, SLOTS, dtype=jnp.int32)
        W = jax.random.normal(k3, (OUT_F, IN_F), dtype=jnp.float32) * 0.02
        b = jax.random.normal(k4, (OUT_F,), dtype=jnp.float32) * 0.02
        lora_As = jax.random.normal(k5, (SLOTS, IN_F, R), dtype=jnp.float32) * 0.02
        lora_Bs = jax.random.normal(k6, (SLOTS, R, OUT_F), dtype=jnp.float32) * 0.02
        return {'x': x, 'adapter_mapping': adapter_mapping, 'W': W, 'b': b, 'lora_As': lora_As, 'lora_Bs': lora_Bs}
    _L0_cond_all = _L0_cond_setup()
    _L0_cond_in = {k: v for k, v in _L0_cond_all.items() if k in ('W', 'b', 'lora_As', 'lora_Bs')}
    del _L0_cond_all

    def _L1_cond_setup():
        import jax, jax.numpy as jnp
        import numpy as np
        B, N, H, F = (4, 64, 512, 1376)
        L, R, RANK = (1, 16, 16)
        SCALE = 0.5
        key = jax.random.key(seed)
        ks = jax.random.split(key, 12)
        nrm = lambda k, shape, fan: jax.random.normal(k, shape, jnp.float32) * fan ** (-0.5)
        inp = {'x': jax.random.normal(ks[0], (B, N, H), jnp.float32), 'W_gate': nrm(ks[1], (F, H), H), 'W_up': nrm(ks[2], (F, H), H), 'W_down': nrm(ks[3], (H, F), F), 'A_gate': nrm(ks[4], (L, R, RANK, H), H), 'B_gate': nrm(ks[5], (L, R, F, RANK), RANK), 'A_up': nrm(ks[6], (L, R, RANK, H), H), 'B_up': nrm(ks[7], (L, R, F, RANK), RANK), 'A_down': nrm(ks[8], (L, R, RANK, F), F), 'B_down': nrm(ks[9], (L, R, H, RANK), RANK), 'lora_indices': jax.random.randint(ks[10], (B,), 0, R), 'layer_idx': 0}
        return inp
    _L1_cond_all = _L1_cond_setup()
    _L1_cond_in = {k: v for k, v in _L1_cond_all.items() if k in ('W_gate', 'W_up', 'W_down', 'A_gate', 'B_gate', 'A_up', 'B_up', 'A_down', 'B_down')}
    del _L1_cond_all
    return {'x': x, 'itok_B_0_23': itok_B_0_23, 'itok_B_2_6': itok_B_2_6, 'L0_cond_W': _L0_cond_in['W'], 'L0_cond_b': _L0_cond_in['b'], 'L0_cond_lora_As': _L0_cond_in['lora_As'], 'L0_cond_lora_Bs': _L0_cond_in['lora_Bs'], 'L1_cond_W_gate': _L1_cond_in['W_gate'], 'L1_cond_W_up': _L1_cond_in['W_up'], 'L1_cond_W_down': _L1_cond_in['W_down'], 'L1_cond_A_gate': _L1_cond_in['A_gate'], 'L1_cond_B_gate': _L1_cond_in['B_gate'], 'L1_cond_A_up': _L1_cond_in['A_up'], 'L1_cond_B_up': _L1_cond_in['B_up'], 'L1_cond_A_down': _L1_cond_in['A_down'], 'L1_cond_B_down': _L1_cond_in['B_down']}

def reference(x, itok_B_0_23, itok_B_2_6, L0_cond_W, L0_cond_b, L0_cond_lora_As, L0_cond_lora_Bs, L1_cond_W_gate, L1_cond_W_up, L1_cond_W_down, L1_cond_A_gate, L1_cond_B_gate, L1_cond_A_up, L1_cond_B_up, L1_cond_A_down, L1_cond_B_down):
    import jax
    import jax.numpy as jnp

    def _L0_cond_ref(x, adapter_mapping, W, b, lora_As, lora_Bs):
        import jax, jax.numpy as jnp
        import numpy as np
        R = 16
        ALPHA = 32
        SCALING = ALPHA / R
        SLOTS = 32
        IN_F = 512
        OUT_F = 512
        B, T = (8, 128)
        base_out = jnp.einsum('bti,oi->bto', x, W) + b
        A = lora_As[adapter_mapping]
        Bm = lora_Bs[adapter_mapping]
        lora_h = jnp.einsum('bti,bir->btr', x, A)
        lora_out = jnp.einsum('btr,bro->bto', lora_h, Bm)
        return base_out + lora_out * SCALING

    def _L1_cond_ref(x, W_gate, W_up, W_down, A_gate, B_gate, A_up, B_up, A_down, B_down, lora_indices, layer_idx):
        import jax, jax.numpy as jnp
        import numpy as np
        B, N, H, F = (4, 64, 512, 1376)
        L, R, RANK = (1, 16, 16)
        SCALE = 0.5

        def lora_add(base, inp, A, B):
            Ab = A[layer_idx][lora_indices]
            Bb = B[layer_idx][lora_indices]
            t = jnp.einsum('bri,bni->bnr', Ab, inp)
            return base + jnp.einsum('bor,bnr->bno', Bb, t) * SCALE
        gate = lora_add(jnp.einsum('bnh,fh->bnf', x, W_gate), x, A_gate, B_gate)
        up = lora_add(jnp.einsum('bnh,fh->bnf', x, W_up), x, A_up, B_up)
        act = jax.nn.silu(gate) * up
        down = lora_add(jnp.einsum('bnf,hf->bnh', act, W_down), act, A_down, B_down)
        return down
    x = x + _L0_cond_ref(x, itok_B_0_23, L0_cond_W, L0_cond_b, L0_cond_lora_As, L0_cond_lora_Bs)
    x = x + _L1_cond_ref(x, L1_cond_W_gate, L1_cond_W_up, L1_cond_W_down, L1_cond_A_gate, L1_cond_B_gate, L1_cond_A_up, L1_cond_B_up, L1_cond_A_down, L1_cond_B_down, itok_B_2_6, 0)
    return x

_drawn_inputs = setup_inputs


def setup_inputs(seed=0):
    import zlib

    import numpy as np

    out = dict(_drawn_inputs(seed))
    spreads = {}
    factors = {'L0_cond_b': 2.825}
    for name, (base, spread) in spreads.items():
        noise = np.random.default_rng([zlib.crc32(name.encode()), seed]).standard_normal(out[name].shape)
        drawn = base * np.exp(spread * noise) if base else spread * noise
        out[name] = jnp.asarray(drawn.astype(out[name].dtype))
    for name, factor in factors.items():
        out[name] = (out[name] * factor).astype(out[name].dtype)
    return out
```

```python
from contextlib import ExitStack

import concourse.bass as bass
from concourse import mybir

P = 128
F32 = mybir.dt.float32
F32R = mybir.dt.float32r
I32 = mybir.dt.int32
ALU = mybir.AluOpType
ACT = mybir.ActivationFunctionType

SEQS, SEQ_LEN, H, F, RANK = 8, 128, 512, 1376, 16
SLOTS0, SLOTS1 = 32, 16
TOKENS = SEQS * SEQ_LEN
HALF = TOKENS // 2
PAIRS = SEQS // 2
PAIR = 2 * SEQ_LEN
KT = H // P
FT = -(-F // P)
F_LAST = F - (FT - 1) * P
BLOCK = 4
BLOCKS = (FT - 1) // BLOCK
TAIL = FT - BLOCKS * BLOCK
BW = 2 * P

STAGE_A = KT // 2
STAGE_F = STAGE_A + 1
STAGE_BF = KT // 2
STAGE_BD = STAGE_BF + FT

C_MASK0, C_MASK1, C_SB, C_LB, C_ST, C_LT = 0, PAIR, 2 * PAIR, 2 * PAIR + 1, 2 * PAIR + 2, 2 * PAIR + 3
C_COLS = 2 * PAIR + 4

CREDIT = 2


def build(nc, xT, idx0, idx1, w0T, bias, a0, b0, wgT, wuT, agu, bgu, wdT, ad, ad_last, bd, consts, outT):
    with ExitStack() as ctx:
        def sb(name, shape, dt=F32):
            return ctx.enter_context(nc.sbuf_tensor(name, shape, dt))

        def bank(name):
            return ctx.enter_context(nc.psum_tensor(name, [P, HALF], F32))

        def sem(name):
            return ctx.enter_context(nc.semaphore(name))

        b0_rows = nc.dram_tensor("b0_rows", (SEQS * RANK, H), F32, kind="Internal").ap()
        bgu_rows = nc.dram_tensor("bgu_rows", (SEQS * RANK, 2 * F), F32, kind="Internal").ap()
        bd_rows = nc.dram_tensor("bd_rows", (SEQS * RANK, H), F32, kind="Internal").ap()

        idx = sb("idx", [1, 2 * SEQS], I32)
        cst = sb("cst", [P, C_COLS])
        bias_sb = sb("bias_sb", [P, KT])
        x = sb("x", [P, KT, TOKENS])
        x1_hi = sb("x1_hi", [P, KT, TOKENS], F32R)
        x1_lo = sb("x1_lo", [P, KT, TOKENS], F32R)
        act_hi = sb("act_hi", [P, BLOCK, TOKENS], F32R)
        act_lo = sb("act_lo", [P, BLOCK, TOKENS], F32R)
        raw_w = sb("raw_w", [P, 2, 2, KT, P])
        w_hi = sb("w_hi", [P, 2, 2, KT, P], F32R)
        w_lo = sb("w_lo", [P, 2, 2, KT, P], F32R)
        raw_agu = sb("raw_agu", [P, SEQS, 2, KT, RANK])
        raw_b = sb("raw_b", [P, 2, PAIRS, 2, P])
        b_x = sb("b_x", [P, 2, PAIRS, 2, P], F32R)
        raw_d = sb("raw_d", [P, 2, BLOCK, P])
        wd_hi = sb("wd_hi", [P, 2, BLOCK, P], F32R)
        wd_lo = sb("wd_lo", [P, 2, BLOCK, P], F32R)
        raw_a = sb("raw_a", [P, SEQS, BLOCK, RANK])
        a_x = sb("a_x", [P, BLOCK, 2, 2, 4 * RANK], F32R)
        t_low = sb("t_low", [P, PAIR])
        t_sum = sb("t_sum", [P, PAIR])
        t_gu = sb("t_gu", [P, PAIR])
        zeros = sb("zeros", [P, HALF], F32R)
        t_rep = sb("t_rep", [P, 2, 2, PAIR])
        t_x = sb("t_x", [P, PAIRS, PAIR], F32R)
        tgu_x = sb("tgu_x", [P, PAIRS, 2, PAIR], F32R)
        sil = sb("sil", [P, 2, HALF])
        act = sb("act", [P, 2, HALF])

        t_bank = [bank("t_bank0"), bank("t_bank1")]
        d_bank = [bank("d_bank0"), bank("d_bank1")]
        gu_bank = [[bank(f"gu_bank{h}{o}") for o in range(2)] for h in range(2)]
        wide = [gu_bank[0][0], gu_bank[0][1], gu_bank[1][0], gu_bank[1][1]]
        l0_bank = wide + [d_bank[0], d_bank[1], wide[0], wide[1]]
        tail_bank = [d_bank[0], d_bank[1]] + wide + [d_bank[0], d_bank[1]]

        idx_in, cst_in = sem("idx_in"), sem("cst_in")
        x_in = [[sem(f"x_in{h}{k}") for k in range(KT)] for h in range(2)]
        w_in = [[sem(f"w_in{s}{o}") for o in range(2)] for s in range(2)]
        agu_in, a0_in, ad_in = sem("agu_in"), sem("a0_in"), sem("ad_in")
        b0_gathered, bgu_gathered, bd_gathered = sem("b0_gathered"), sem("bgu_gathered"), sem("bd_gathered")
        b_in = [sem("b_in0"), sem("b_in1")]
        d_in = [sem("d_in0"), sem("d_in1")]
        w_hi_ok, w_ok, w_free = sem("w_hi_ok"), sem("w_ok"), sem("w_free")
        w0_hi_ok, w0_ok = sem("w0_hi_ok"), sem("w0_ok")
        b_hi_ok, b_ok = sem("b_hi_ok"), sem("b_ok")
        d_hi_ok, d_ok, d_free = sem("d_hi_ok"), sem("d_ok"), sem("d_free")
        a_hi_ok, a_ok, a_free = sem("a_hi_ok"), sem("a_ok"), sem("a_free")
        x_hi_ok, x_lo_dve, x_lo_pool = sem("x_hi_ok"), sem("x_lo_dve"), sem("x_lo_pool")
        t_psum_ok, t_step, t_rep_ok, t_hi_ok, t_ok = (
            sem("t_psum_ok"), sem("t_step"), sem("t_rep_ok"), sem("t_hi_ok"), sem("t_ok"))
        l0_ok, x1_ok, x1_hi_ok, x1_lo_ok = sem("l0_ok"), sem("x1_ok"), sem("x1_hi_ok"), sem("x1_lo_ok")
        gate_ok, up_ok, silu_ok, act_ok = sem("gate_ok"), sem("up_ok"), sem("silu_ok"), sem("act_ok")
        act_hi_ok, act_lo_ok = sem("act_hi_ok"), sem("act_lo_ok")
        down_ok, added = sem("down_ok"), sem("added")
        zeros_ok, out_done = sem("zeros_ok"), sem("out_done")

        def cols(h):
            return slice(h * HALF, (h + 1) * HALF)

        def f32(ap):
            return ap.bitcast(F32)

        def w_in_count(s):
            return 16 * (s // 2 + 1 - (1 if s % 2 == STAGE_A % 2 else 0)) if s > STAGE_A else 16

        def f_in_count(b, j):
            return b * (16 * BLOCK // 2) + w_in_count(STAGE_F + j)

        def b_in_count(b, j):
            return b * (64 * BLOCK // 2) + 64 * ((STAGE_BF + j) // 2 + 1)

        def w_slot(j):
            return (STAGE_F + j) % 2

        def b_slot(j):
            return (STAGE_BF + j) % 2

        def agu_views(w, s):
            half, a, e = s // 4, s % 4 // 2, s % 2
            to = w[:, STAGE_A % 2, half, :, 64 * a:64 * a + 64].rearrange("p k (o e r) -> p k o e r", o=2, e=2)
            return to[:, :, :, e, :], raw_agu[:, s].rearrange("p o k r -> p k o r")

        def a_part(h, part):
            return a_x[:, :, h, part, :].rearrange("p k (s r) -> p k s r", s=SEQS // 2)

        def a_whole(h):
            return raw_a[:, h * SEQS // 2:(h + 1) * SEQS // 2].rearrange("p s k r -> p k s r")

        block = ctx.enter_context(nc.Block())

        @block.sync
        def _(sp):
            sp.dma_start(idx[:, 0:SEQS], idx0).then_inc(idx_in, 16)
            sp.dma_start(idx[:, SEQS:], idx1).then_inc(idx_in, 16)

            def load_w0(s):
                for o in range(2):
                    sp.dma_start(raw_w[:, s, o, :, :], w0T[2 * s + o]).then_inc(w_in[s][o], 16)

            def load_b(slot, rows, c0, width, done):
                for q in range(4):
                    src = rows[:, bass.ds(c0, width)].rearrange("(a p) f -> p a f", a=PAIRS)
                    dst = raw_b[32 * q:32 * q + 32, slot, :, :, :].rearrange("p a o f -> p a (o f)")
                    sp.dma_start(dst[:, :, 0:width], src).then_inc(done, 16)

            load_w0(0)
            sp.wait_ge(idx_in, 32)
            slot0 = [sp.value_load(idx[0:1, s:s + 1], min_val=0, max_val=SLOTS0 - 1) for s in range(SEQS)]
            for s in range(SEQS):
                sp.dma_start(b0_rows[s * RANK:(s + 1) * RANK, :],
                             b0[bass.ds(slot0[s], 1)].rearrange("a r f -> (a r) f")).then_inc(b0_gathered, 16)
            for s in range(SEQS):
                sp.dma_start(raw_a[:, s, :, :],
                             a0[bass.ds(slot0[s], 1)].rearrange("a p k r -> (a p) k r")).then_inc(a0_in, 16)
            load_w0(1)
            sp.wait_ge(b0_gathered, 16 * SEQS)
            load_b(0, b0_rows, 0, BW, b_in[0])
            load_b(1, b0_rows, BW, BW, b_in[1])

            slot1 = [sp.value_load(idx[0:1, SEQS + s:SEQS + s + 1], min_val=0, max_val=SLOTS1 - 1)
                     for s in range(SEQS)]
            for s in range(SEQS):
                sp.dma_start(raw_agu[:, s, :, :, :],
                             agu[bass.ds(slot1[s], 1)].rearrange("a p o k r -> (a p) o k r")).then_inc(agu_in, 16)
            for s in range(SEQS):
                sp.dma_start(bgu_rows[s * RANK:(s + 1) * RANK, :],
                             bgu[bass.ds(slot1[s], 1)].rearrange("a r f -> (a r) f")).then_inc(bgu_gathered, 16)
                sp.dma_start(bd_rows[s * RANK:(s + 1) * RANK, :],
                             bd[bass.ds(slot1[s], 1)].rearrange("a r f -> (a r) f")).then_inc(bd_gathered, 16)
            sp.wait_ge(bgu_gathered, 16 * SEQS)

            def load_f_tile(b, j):
                t = b * BLOCK + j
                last = j == TAIL - 1 and isinstance(b, int)
                width = F_LAST if last else P
                sp.wait_ge(w_ok, t + (STAGE_F - 1))
                for o, w in ((0, wgT), (1, wuT)):
                    src = w[:, bass.ds(t * P, width)].rearrange("(k p) f -> p k f", p=P)
                    sp.dma_start(raw_w[:, w_slot(j), o, :, 0:width], src).then_inc(w_in[w_slot(j)][o], 16)
                sp.wait_ge(b_ok, t + (STAGE_BF - 1))
                if not last:
                    load_b(b_slot(j), bgu_rows, t * BW, BW, b_in[b_slot(j)])
                else:
                    for q in range(4):
                        for o in range(2):
                            src = bgu_rows[:, t * BW + o * width:t * BW + (o + 1) * width]
                            sp.dma_start(raw_b[32 * q:32 * q + 32, b_slot(j), :, o, 0:width],
                                         src.rearrange("(a p) f -> p a f", a=PAIRS)).then_inc(b_in[b_slot(j)], 16)

            def load_down(b, tiles):
                tail = isinstance(b, int)
                sp.wait_ge(a_ok, b + 1)
                for s in range(SEQS):
                    whole = tiles - 1 if tail else tiles
                    src = ad[bass.ds(slot1[s], 1), :, bass.ds(b * BLOCK, whole), :]
                    sp.dma_start(raw_a[:, s, 0:whole, :], src.rearrange("a p k r -> (a p) k r")).then_inc(ad_in, 16)
                    if tail:
                        src = ad_last[bass.ds(slot1[s], 1)].rearrange("a p r -> (a p) r")
                        sp.dma_start(raw_a[0:F_LAST, s, whole, :], src).then_inc(ad_in, 16)
                for ht in range(KT):
                    sp.wait_ge(d_ok, b * KT + (ht + 1))
                    f0 = b * (BLOCK * P)
                    if not tail:
                        src = wdT[bass.ds(f0, tiles * P), ht * P:(ht + 1) * P].rearrange("(k p) f -> p k f", p=P)
                        sp.dma_start(raw_d[:, ht % 2, :, :], src).then_inc(d_in[ht % 2], 16)
                    else:
                        whole = tiles - 1
                        src = wdT[f0:f0 + whole * P, ht * P:(ht + 1) * P].rearrange("(k p) f -> p k f", p=P)
                        sp.dma_start(raw_d[:, ht % 2, 0:whole, :], src).then_inc(d_in[ht % 2], 16)
                        sp.dma_start(raw_d[0:F_LAST, ht % 2, whole, :],
                                     wdT[f0 + whole * P:F, ht * P:(ht + 1) * P]).then_inc(d_in[ht % 2], 16)

            with sp.Fori(0, BLOCKS) as b:
                for j in range(BLOCK):
                    load_f_tile(b, j)
                load_down(b, BLOCK)
            for j in range(TAIL):
                load_f_tile(BLOCKS, j)
            load_down(BLOCKS, TAIL)
            sp.wait_ge(bd_gathered, 16 * SEQS)
            for o in range(KT // 2):
                sp.wait_ge(b_ok, STAGE_BD + o - 1)
                load_b((STAGE_BD + o) % 2, bd_rows, o * BW, BW, b_in[(STAGE_BD + o) % 2])
            for ht in range(KT):
                for h in range(2):
                    sp.wait_ge(added, CREDIT + BLOCKS * 2 * KT + 2 * ht + h + 1)
                    sp.dma_start(outT[ht, :, cols(h)], x[:, ht, cols(h)]).then_inc(out_done, 16)
            sp.wait_ge(out_done, 16 * 2 * KT)

        @block.scalar
        def _(eng):
            eng.sem_inc(silu_ok, CREDIT)
            for k in range(KT):
                eng.dma_start(x[:, k, cols(0)], xT[0, k]).then_inc(x_in[0][k], 16)
            eng.dma_start(cst[:, :], consts).then_inc(cst_in, 16)
            eng.dma_start(bias_sb[:, :], bias).then_inc(cst_in, 16)
            for k in range(KT):
                eng.dma_start(x[:, k, cols(1)], xT[1, k]).then_inc(x_in[1][k], 16)

            def round_to(out, in_, scale=1.0):
                return eng.activation(out, in_, ACT.Copy, scale=scale)

            def x_hi(h, k):
                eng.wait_ge(x_in[h][k], 16)
                round_to(act_hi[:, k, cols(h)], x[:, k, cols(h)]).then_inc(x_hi_ok, 1)

            def w_hi_part(slot):
                round_to(w_hi[:, slot], raw_w[:, slot]).then_inc(w_hi_ok, 1)

            def b_hi_part(slot):
                round_to(b_x[:, slot], raw_b[:, slot], cst[:, C_SB:C_SB + 1]).then_inc(b_hi_ok, 1)

            def a_hi_part():
                for h in range(2):
                    last = round_to(a_part(h, 0), a_whole(h))
                last.then_inc(a_hi_ok, 1)

            def t_hi_part(n, out, in_):
                eng.wait_ge(t_rep_ok, n)
                round_to(out, in_, cst[:, C_ST:C_ST + 1]).then_inc(t_hi_ok, 1)

            def x1_hi_part(h, ot):
                eng.wait_ge(x1_ok, h * KT + ot + 1)
                round_to(x1_hi[:, ot, cols(h)], x[:, ot, cols(h)]).then_inc(x1_hi_ok, 1)

            eng.wait_ge(w_in[0][0], 16)
            round_to(w_hi[:, 0, 0], raw_w[:, 0, 0]).then_inc(w0_hi_ok, 1)
            for k in range(KT):
                x_hi(0, k)
            eng.wait_ge(w_in[0][1], 16)
            round_to(w_hi[:, 0, 1], raw_w[:, 0, 1]).then_inc(w_hi_ok, 1)
            eng.wait_ge(a0_in, 16 * SEQS)
            a_hi_part()
            eng.wait_ge(w_in[1][0], 16)
            eng.wait_ge(w_in[1][1], 16)
            w_hi_part(1)
            for k in range(KT):
                x_hi(1, k)
            eng.wait_ge(cst_in, 32)
            for s in range(2):
                eng.wait_ge(b_in[s], 64)
                b_hi_part(s)
            for h in range(2):
                t_hi_part(h + 1, t_x[:, 2 * h:2 * h + 2, :], t_rep[:, 0])
                for ot in range(2):
                    x1_hi_part(0, 2 * h + ot)
            x1_hi_part(1, 0)
            x1_hi_part(1, 1)
            eng.wait_ge(agu_in, 16 * SEQS)
            eng.wait_ge(w_free, 1)
            for s in range(SEQS):
                dst, src = agu_views(w_hi, s)
                last = round_to(dst, src)
            last.then_inc(w_hi_ok, 1)
            x1_hi_part(1, 2)
            x1_hi_part(1, 3)

            def w_f_hi(b, j):
                for o in range(2):
                    eng.wait_ge(w_in[w_slot(j)][o], f_in_count(b, j))
                eng.wait_ge(w_free, b * BLOCK + (STAGE_F + j - 1))
                w_hi_part(w_slot(j))

            def b_f_hi(b, j, more=0):
                eng.wait_ge(b_in[b_slot(j)], b_in_count(b, j) + more)
                if j > 0:
                    eng.wait_ge(up_ok, b * (2 * BLOCK) + 2 * j)
                b_hi_part(b_slot(j))

            def a_d_hi(b, landed):
                eng.wait_ge(ad_in, landed)
                eng.wait_ge(a_free, b + 1)
                a_hi_part()

            def d_hi_part(b, ht, landed):
                eng.wait_ge(d_in[ht % 2], landed)
                if ht >= 2 and isinstance(b, int):
                    eng.wait_ge(d_free, ht - 1)
                elif ht >= 2:
                    eng.wait_ge(down_ok, b * (2 * KT) + (2 * ht - 2))
                round_to(wd_hi[:, ht % 2], raw_d[:, ht % 2]).then_inc(d_hi_ok, 1)

            def gate_tile(b, j, rows):
                for h in range(2):
                    n = 2 * (b * BLOCK + j) + h
                    eng.wait_ge(gate_ok, n + 1)
                    eng.wait_ge(act_ok, n + 1)
                    eng.activation(sil[0:rows, h], gu_bank[h][0][0:rows], ACT.Silu).then_inc(silu_ok, 1)
                for h in range(2):
                    n = 2 * (b * BLOCK + j) + h
                    eng.wait_ge(act_ok, CREDIT + n + 1)
                    round_to(act_hi[0:rows, j, cols(h)], act[0:rows, h]).then_inc(act_hi_ok, 1)

            w_f_hi(0, 0)
            b_f_hi(0, 0)
            for h in range(2):
                t_hi_part(3 + h, tgu_x[:, 2 * h:2 * h + 2, :, :],
                          t_rep[:, :, :, :].rearrange("p o a t -> p a o t"))

            with eng.Fori(0, BLOCKS) as b:
                for j in range(BLOCK):
                    if j + 1 < BLOCK:
                        w_f_hi(b, j + 1)
                        b_f_hi(b, j + 1)
                    if j == 2:
                        a_d_hi(b, 16 * SEQS * (b + 1))
                    if j == 3:
                        for ht in range(2):
                            d_hi_part(b, ht, 32 * b + 16)
                    gate_tile(b, j, P)
                w_f_hi(b, BLOCK)
                b_f_hi(b, BLOCK)
                for ht in range(2, KT):
                    d_hi_part(b, ht, 32 * b + 32)
            d_base = 32 * BLOCKS
            for j in range(TAIL):
                if j + 1 < TAIL:
                    w_f_hi(BLOCKS, j + 1)
                    b_f_hi(BLOCKS, j + 1, 64 if j + 1 == TAIL - 1 else 0)
                if j == 1:
                    a_d_hi(BLOCKS, 16 * SEQS * (BLOCKS + 2))
                    d_hi_part(BLOCKS, 0, d_base + 32)
                if j == 2:
                    d_hi_part(BLOCKS, 1, d_base + 32)
                gate_tile(BLOCKS, j, P if j + 1 < TAIL else F_LAST)
            for o in range(KT // 2):
                b_f_hi(BLOCKS, TAIL + o, 64 if (STAGE_BD + o) % 2 == b_slot(TAIL - 1) else 0)
            for h in range(2):
                t_hi_part(5 + h, t_x[:, 2 * h:2 * h + 2, :], t_rep[:, 0])
            for ht in range(2, KT):
                d_hi_part(BLOCKS, ht, d_base + 64)

        @block.vector
        def _(eng):
            eng.sem_inc(act_ok, CREDIT)
            eng.sem_inc(d_ok, CREDIT)
            eng.sem_inc(added, CREDIT)

            def minus(out, whole, hi):
                return eng.tensor_tensor(out, whole, f32(hi), ALU.subtract)

            def x_lo(n, k):
                eng.wait_ge(x_hi_ok, n)
                minus(act_lo[:, k, cols(0)], x[:, k, cols(0)], act_hi[:, k, cols(0)]).then_inc(x_lo_dve, 1)

            def w_lo_part(n, slot):
                eng.wait_ge(w_hi_ok, n)
                minus(w_lo[:, slot], raw_w[:, slot], w_hi[:, slot]).then_inc(w_ok, 1)

            def b_lo_part(n, slot):
                eng.wait_ge(b_hi_ok, n)
                eng.scalar_tensor_tensor(out=b_x[:, slot].rearrange("p a o f -> p (a o f)"),
                                         in0=raw_b[:, slot].rearrange("p a o f -> p (a o f)"),
                                         scalar=cst[:, C_LB:C_LB + 1],
                                         in1=f32(b_x[:, slot].rearrange("p a o f -> p (a o f)")),
                                         op0=ALU.mult, op1=ALU.add).then_inc(b_ok, 1)

            def a_lo_part(n):
                eng.wait_ge(a_hi_ok, n)
                for h in range(2):
                    last = minus(a_part(h, 1), a_whole(h), a_part(h, 0))
                last.then_inc(a_ok, 1)

            steps = [0]

            def step(op):
                op.then_inc(t_step, 1)
                steps[0] += 1

            def all_steps():
                eng.wait_ge(t_step, steps[0])

            def t_summed(n, h, mask):
                eng.wait_ge(t_psum_ok, n)
                ps = t_bank[h]
                for a in range(2):
                    row, col = slice(32 * a, 32 * a + 32), slice(a * PAIR, (a + 1) * PAIR)
                    step(eng.tensor_copy(t_low[row, :], ps[64 + 32 * a:96 + 32 * a, col]))
                all_steps()
                for a in range(2):
                    row, col = slice(32 * a, 32 * a + 32), slice(a * PAIR, (a + 1) * PAIR)
                    step(eng.tensor_tensor(t_sum[row, :], ps[row, col], t_low[row, :], ALU.add))
                all_steps()
                for a in range(2):
                    row = slice(32 * a, 32 * a + 32)
                    for q in range(4):
                        last = eng.tensor_tensor(t_rep[32 * q:32 * q + 32, 0, a, :], t_sum[row, :],
                                                 cst[row, mask:mask + PAIR], ALU.mult)
                last.then_inc(t_rep_ok, 1)

            def t_gate_up(n, h):
                eng.wait_ge(t_psum_ok, n)
                for a in range(2):
                    col = slice(a * PAIR, (a + 1) * PAIR)
                    row = slice(64 * a, 64 * a + 64)
                    step(eng.tensor_tensor(t_gu[row, :], d_bank[h][row, col], cst[row, C_MASK1:C_MASK1 + PAIR],
                                           ALU.mult))
                all_steps()
                for a in range(2):
                    for o in range(2):
                        from_row = slice(64 * a + 32 * o, 64 * a + 32 * o + 32)
                        for q in range(4):
                            last = eng.tensor_copy(t_rep[32 * q:32 * q + 32, o, a, :], t_gu[from_row, :])
                last.then_inc(t_rep_ok, 1)

            def t_lo_part(n, out, in_):
                eng.wait_ge(t_hi_ok, n)
                eng.scalar_tensor_tensor(out=out, in0=in_, scalar=cst[:, C_LT:C_LT + 1], in1=f32(out),
                                         op0=ALU.mult, op1=ALU.add).then_inc(t_ok, 1)

            def t_lo_of_half(n, h):
                t_lo_part(n, t_x[:, 2 * h:2 * h + 2, :].rearrange("p a t -> p (a t)"),
                          t_rep[:, 0].rearrange("p a t -> p (a t)"))

            def x1_part(h, ot):
                eng.wait_ge(l0_ok, h * KT + ot + 1)
                eng.scalar_tensor_tensor(out=x[:, ot, cols(h)], in0=l0_bank[h * KT + ot][:, :],
                                         scalar=bias_sb[:, ot:ot + 1], in1=x[:, ot, cols(h)],
                                         op0=ALU.add, op1=ALU.add).then_inc(x1_ok, 1)

            eng.wait_ge(w0_hi_ok, 1)
            minus(w_lo[:, 0, 0], raw_w[:, 0, 0], w_hi[:, 0, 0]).then_inc(w0_ok, 1)
            x_lo(1, 0)
            x_lo(3, 2)
            eng.wait_ge(w_hi_ok, 1)
            minus(w_lo[:, 0, 1], raw_w[:, 0, 1], w_hi[:, 0, 1]).then_inc(w_ok, 1)
            a_lo_part(1)
            w_lo_part(2, 1)
            b_lo_part(1, 0)
            b_lo_part(2, 1)
            for h in range(2):
                t_summed(h + 1, h, C_MASK0)
                t_lo_of_half(h + 1, h)
                for ot in range(2):
                    x1_part(0, 2 * h + ot)
            x1_part(1, 0)
            x1_part(1, 1)
            eng.wait_ge(w_hi_ok, STAGE_A + 1)
            for s in range(SEQS):
                hi, src = agu_views(w_hi, s)
                dst, _ = agu_views(w_lo, s)
                last = minus(dst, src, hi)
            last.then_inc(w_ok, 1)
            x1_part(1, 2)
            x1_part(1, 3)

            def w_f_lo(b, j):
                w_lo_part(b * BLOCK + (STAGE_F + j + 1), w_slot(j))

            def b_f_lo(b, j):
                b_lo_part(b * BLOCK + (STAGE_BF + j + 1), b_slot(j))

            def d_lo_part(b, ht):
                eng.wait_ge(d_hi_ok, b * KT + (ht + 1))
                minus(wd_lo[:, ht % 2], raw_d[:, ht % 2], wd_hi[:, ht % 2]).then_inc(d_ok, 1)

            def up_tile(b, j, rows):
                for h in range(2):
                    n = 2 * (b * BLOCK + j) + h
                    eng.wait_ge(up_ok, CREDIT + n + 1)
                    eng.wait_ge(silu_ok, CREDIT + n + 1)
                    eng.wait_ge(act_lo_ok, n + 1)
                    eng.tensor_tensor(act[0:rows, h], gu_bank[h][1][0:rows], sil[0:rows, h],
                                      ALU.mult).then_inc(act_ok, 1)

            def add_down(b, ht, banks):
                for h in range(2):
                    eng.wait_ge(down_ok, b * (2 * KT) + (2 * ht + h + 1))
                    eng.tensor_tensor(x[:, ht, cols(h)], banks[h][:, :], x[:, ht, cols(h)],
                                      ALU.add).then_inc(added, 1)

            w_f_lo(0, 0)
            b_f_lo(0, 0)
            for h in range(2):
                t_gate_up(3 + h, h)
                for a in range(2):
                    eng.wait_ge(t_hi_ok, 3 + h)
                    last = eng.scalar_tensor_tensor(
                        out=tgu_x[:, 2 * h + a, :, :], in0=t_rep[:, :, a, :], scalar=cst[:, C_LT:C_LT + 1],
                        in1=f32(tgu_x[:, 2 * h + a, :, :]), op0=ALU.mult, op1=ALU.add)
                last.then_inc(t_ok, 1)

            with eng.Fori(0, BLOCKS) as b:
                for j in range(BLOCK):
                    if j + 1 < BLOCK:
                        w_f_lo(b, j + 1)
                        b_f_lo(b, j + 1)
                    if j == 2:
                        a_lo_part(b + 2)
                    if j == 3:
                        d_lo_part(b, 0)
                        d_lo_part(b, 1)
                    up_tile(b, j, P)
                w_f_lo(b, BLOCK)
                b_f_lo(b, BLOCK)
                for ht in range(KT):
                    add_down(b, ht, d_bank)
                    if ht + 2 < KT:
                        d_lo_part(b, ht + 2)
            for j in range(TAIL):
                if j + 1 < TAIL:
                    w_f_lo(BLOCKS, j + 1)
                    b_f_lo(BLOCKS, j + 1)
                if j == 1:
                    a_lo_part(BLOCKS + 2)
                    d_lo_part(BLOCKS, 0)
                if j == 2:
                    d_lo_part(BLOCKS, 1)
                up_tile(BLOCKS, j, P if j + 1 < TAIL else F_LAST)
            for o in range(KT // 2):
                b_f_lo(BLOCKS, TAIL + o)
            for h in range(2):
                t_summed(5 + h, h, C_MASK1)
                t_lo_of_half(5 + h, h)
            for ht in range(KT):
                if ht < 2:
                    d_lo_part(BLOCKS, ht + 2)
                add_down(BLOCKS, ht, tail_bank[2 * ht:2 * ht + 2])

        @block.gpsimd
        def _(eng):
            eng.sem_inc(act_lo_ok, CREDIT)
            eng.memset(f32(zeros[:, :]), 0.0).then_inc(zeros_ok, 1)

            def minus(out, whole, hi):
                return eng.tensor_tensor(out, whole, f32(hi), ALU.subtract)

            for h, k in [(0, 1), (0, 3)] + [(1, k) for k in range(KT)]:
                eng.wait_ge(x_hi_ok, h * KT + k + 1)
                minus(act_lo[:, k, cols(h)], x[:, k, cols(h)], act_hi[:, k, cols(h)]).then_inc(x_lo_pool, 1)
            for h in range(2):
                for ot in range(KT):
                    eng.wait_ge(x1_hi_ok, h * KT + ot + 1)
                    minus(x1_lo[:, ot, cols(h)], x[:, ot, cols(h)], x1_hi[:, ot, cols(h)]).then_inc(x1_lo_ok, 1)

            def act_lo_tile(b, j, rows):
                for h in range(2):
                    eng.wait_ge(act_hi_ok, 2 * (b * BLOCK + j) + h + 1)
                    minus(act_lo[0:rows, j, cols(h)], act[0:rows, h],
                          act_hi[0:rows, j, cols(h)]).then_inc(act_lo_ok, 1)

            with eng.Fori(0, BLOCKS) as b:
                for j in range(BLOCK):
                    act_lo_tile(b, j, P)
            for j in range(TAIL):
                act_lo_tile(BLOCKS, j, P if j + 1 < TAIL else F_LAST)

        @block.tensor
        def _(eng):
            eng.sem_inc(up_ok, CREDIT)

            def split_product(out, hi, lo, in_hi, in_lo, start, stop=False):
                eng.matmul(out, hi, in_hi, start=start, stop=False)
                eng.matmul(out, hi, in_lo, start=False, stop=False)
                return eng.matmul(out, lo, in_hi, start=False, stop=stop)

            def wide_sum(out, slot, o, in_hi, in_lo, h, stop=False):
                for k in range(KT):
                    last = split_product(out, w_hi[:, slot, o, k, :], w_lo[:, slot, o, k, :],
                                         in_hi[:, k, cols(h)], in_lo[:, k, cols(h)], k == 0,
                                         stop and k == KT - 1)
                return last

            def lora(out, slot, o, t, h):
                for a in range(2):
                    last = eng.matmul(out[:, a * PAIR:(a + 1) * PAIR], b_x[:, slot, 2 * h + a, o, :],
                                      t[:, 2 * h + a, :], start=False, stop=a == 1)
                return last

            def l0_main(h, ot):
                return wide_sum(l0_bank[h * KT + ot][:, :], ot // 2, ot % 2, act_hi, act_lo, h)

            def project(out, h, n_k, start, first, k_rows=P, stop=True):
                for k in range(n_k):
                    if first is not None:
                        eng.wait_ge(act_lo_ok, first + 2 * k)
                    rows = slice(0, k_rows if k == n_k - 1 else P)
                    for v in (act_hi, act_lo):
                        last = eng.matmul(out, a_x[rows, k, h, :, :].rearrange("p v c -> p (v c)"),
                                          v[rows, k, cols(h)], start=start and k == 0 and v is act_hi,
                                          stop=stop and k == n_k - 1 and v is act_lo)
                return last

            def l0_lora(h, ot):
                return lora(l0_bank[h * KT + ot], ot // 2, ot % 2, t_x, h).then_inc(l0_ok, 1)

            eng.wait_ge(w0_ok, 1)
            for k in range(KT):
                if k % 2 == 0:
                    eng.wait_ge(x_lo_dve, k // 2 + 1)
                else:
                    eng.wait_ge(x_lo_pool, k // 2 + 1)
                split_product(l0_bank[0][:, :], w_hi[:, 0, 0, k, :], w_lo[:, 0, 0, k, :],
                              act_hi[:, k, cols(0)], act_lo[:, k, cols(0)], k == 0)
            eng.wait_ge(a_ok, 1)
            project(t_bank[0][:, :], 0, KT, True, None).then_inc(t_psum_ok, 1)
            eng.wait_ge(w_ok, 1)
            l0_main(0, 1)
            eng.wait_ge(w_ok, 2)
            l0_main(0, 2)
            eng.wait_ge(t_ok, 1)
            eng.wait_ge(b_ok, 1)
            l0_lora(0, 0)
            l0_lora(0, 1)
            eng.wait_ge(x_lo_pool, 2 + KT)
            project(t_bank[1][:, :], 1, KT, True, None).then_inc(t_psum_ok, 1)
            eng.sem_inc(a_free, 1)
            l0_main(0, 3)
            eng.wait_ge(b_ok, 2)
            l0_lora(0, 2)
            l0_lora(0, 3)
            for ot in range(KT):
                if ot >= 2:
                    eng.wait_ge(x1_ok, ot - 1)
                last = l0_main(1, ot)
                if ot % 2:
                    last.then_inc(w_free, 1)
                if ot == 0:
                    eng.wait_ge(t_ok, 2)
                l0_lora(1, ot)

            for h in range(2):
                eng.wait_ge(x1_ok, KT + h + 1)
                eng.wait_ge(x1_lo_ok, (h + 1) * KT)
                if h == 0:
                    eng.wait_ge(w_ok, STAGE_A + 1)
                last = wide_sum(d_bank[h][:, :], STAGE_A % 2, h, x1_hi, x1_lo, h, stop=True)
                last.then_inc(t_psum_ok, 1)
            eng.wait_ge(zeros_ok, 1)
            for h in range(2):
                eng.matmul(t_bank[h][:, :], zeros[:, 0:P], zeros[:, :], start=True, stop=False)

            def f_tile(b, j, last_tile=False):
                width = F_LAST if last_tile else P
                t = b * BLOCK + j
                ws, bs = w_slot(j), b_slot(j)
                eng.wait_ge(w_ok, t + (STAGE_F + 1))
                for h in range(2):
                    n = 2 * t + h
                    for o in range(2):
                        eng.wait_ge((silu_ok, act_ok)[o], n + 1)
                        for k in range(KT):
                            last = split_product(gu_bank[h][o][0:width, :], w_hi[:, ws, o, k, 0:width],
                                                 w_lo[:, ws, o, k, 0:width], x1_hi[:, k, cols(h)],
                                                 x1_lo[:, k, cols(h)], k == 0)
                    if h == 1:
                        last.then_inc(w_free, 1)
                    else:
                        eng.wait_ge(b_ok, t + (STAGE_BF + 1))
                    eng.wait_ge(t_ok, 3 + h)
                    for o in range(2):
                        for a in range(2):
                            last = eng.matmul(gu_bank[h][o][0:width, a * PAIR:(a + 1) * PAIR],
                                              b_x[:, bs, 2 * h + a, o, 0:width], tgu_x[:, 2 * h + a, o, :],
                                              start=False, stop=a == 1)
                        last.then_inc((gate_ok, up_ok)[o], 1)

            def down_sum(out, ht, h, n_k, k_rows=P, stop=True):
                for k in range(n_k):
                    rows = slice(0, k_rows if k == n_k - 1 else P)
                    last = split_product(out, wd_hi[rows, ht % 2, k, :], wd_lo[rows, ht % 2, k, :],
                                         act_hi[rows, k, cols(h)], act_lo[rows, k, cols(h)], k == 0,
                                         stop and k == n_k - 1)
                return last

            with eng.Fori(0, BLOCKS) as b:
                for j in range(BLOCK):
                    f_tile(b, j)
                eng.wait_ge(a_ok, b + 2)
                for h in range(2):
                    last = project(t_bank[h][:, :], h, BLOCK, False, b * (2 * BLOCK) + (CREDIT + h + 1),
                                   stop=False)
                last.then_inc(a_free, 1)
                for ht in range(KT):
                    eng.wait_ge(d_ok, b * KT + (CREDIT + ht + 1))
                    for h in range(2):
                        eng.wait_ge(added, b * (2 * KT) + (2 * ht + h + 1))
                        down_sum(d_bank[h][:, :], ht, h, BLOCK).then_inc(down_ok, 1)
            for j in range(TAIL):
                f_tile(BLOCKS, j, j == TAIL - 1)

            eng.wait_ge(a_ok, BLOCKS + 2)
            for h in range(2):
                project(t_bank[h][:, :], h, TAIL, False, BLOCKS * 2 * BLOCK + CREDIT + h + 1,
                        F_LAST).then_inc(t_psum_ok, 1)

            def down_lora(n):
                ht, h = n // 2, n % 2
                if n < 2:
                    eng.wait_ge(t_ok, 5 + n)
                eng.wait_ge(b_ok, STAGE_BD + ht // 2 + 1)
                lora(tail_bank[n], (STAGE_BD + ht // 2) % 2, ht % 2, t_x, h).then_inc(down_ok, 1)

            LAG = 3
            for n in range(2 * KT + LAG):
                if n < 2 * KT:
                    ht, h = n // 2, n % 2
                    eng.wait_ge(d_ok, BLOCKS * KT + CREDIT + ht + 1)
                    if n < 2:
                        eng.wait_ge(added, BLOCKS * 2 * KT + n + 1)
                    elif n >= 6:
                        eng.wait_ge(added, BLOCKS * 2 * KT + CREDIT + n - 5)
                    last = down_sum(tail_bank[n][:, :], ht, h, TAIL, F_LAST, stop=False)
                    if h == 1:
                        last.then_inc(d_free, 1)
                if n >= LAG:
                    down_lora(n - LAG)


def kernel(x, itok_B_0_23, itok_B_2_6, L0_cond_W, L0_cond_b, L0_cond_lora_As, L0_cond_lora_Bs, L1_cond_W_gate,
           L1_cond_W_up, L1_cond_W_down, L1_cond_A_gate, L1_cond_B_gate, L1_cond_A_up, L1_cond_B_up,
           L1_cond_A_down, L1_cond_B_down):
    import numpy as np
    import concourse.bacc as bacc
    from concourse.bass_utils import run_bass_kernel_spmd

    def tiles(a):
        return a.reshape(a.shape[0], -1, P, a.shape[-1]).transpose(0, 2, 1, 3)

    p, t = np.arange(P), np.arange(PAIR)
    same = (p[:, None] % 32 // RANK == t[None, :] // SEQ_LEN).astype(np.float32)
    b_low, t_low = (p // 32 % 2).astype(np.float32), (p // 64).astype(np.float32)
    consts = np.concatenate([same * 2.0, same * 0.5, np.stack([1 - 2 * b_low, b_low, 1 - 2 * t_low, t_low], 1)],
                            axis=1).astype(np.float32)

    whole = (FT - 1) * P
    b_gate, b_up = (a[0].transpose(0, 2, 1) for a in (L1_cond_B_gate, L1_cond_B_up))
    b_gu = np.stack([b_gate[:, :, :whole].reshape(SLOTS1, RANK, FT - 1, P),
                     b_up[:, :, :whole].reshape(SLOTS1, RANK, FT - 1, P)], axis=3)
    b_last = np.stack([b_gate[:, :, whole:], b_up[:, :, whole:]], axis=2)
    arrays = {
        "xT": x.reshape(2, HALF, KT, P).transpose(0, 2, 3, 1),
        "idx0": itok_B_0_23.reshape(1, SEQS),
        "idx1": itok_B_2_6.reshape(1, SEQS),
        "w0T": L0_cond_W.reshape(KT, P, KT, P).transpose(0, 3, 2, 1),
        "bias": L0_cond_b.reshape(KT, P).T,
        "a0": tiles(L0_cond_lora_As),
        "b0": L0_cond_lora_Bs,
        "wgT": L1_cond_W_gate.T,
        "wuT": L1_cond_W_up.T,
        "agu": np.stack([tiles(a[0].transpose(0, 2, 1)) for a in (L1_cond_A_gate, L1_cond_A_up)], axis=2),
        "bgu": np.concatenate([b_gu.reshape(SLOTS1, RANK, -1),
                               b_last.reshape(SLOTS1, RANK, -1)], axis=2),
        "wdT": L1_cond_W_down.T,
        "ad": tiles(L1_cond_A_down[0].transpose(0, 2, 1)[:, :whole]),
        "ad_last": L1_cond_A_down[0].transpose(0, 2, 1)[:, whole:],
        "bd": L1_cond_B_down[0].transpose(0, 2, 1),
        "consts": consts,
    }
    arrays = {name: np.ascontiguousarray(a) for name, a in arrays.items()}
    nc = bacc.Bacc("TRN2", target_bir_lowering=False, num_devices=1)
    ins = {name: nc.dram_tensor(name, a.shape, mybir.dt.from_np(a.dtype), kind="ExternalInput").ap()
           for name, a in arrays.items()}
    outT = nc.dram_tensor("outT", (KT, P, TOKENS), F32, kind="ExternalOutput").ap()
    build(nc, outT=outT, **ins)
    result = run_bass_kernel_spmd(nc, [arrays], core_ids=[0])
    return result.results[0]["outT"].reshape(H, TOKENS).T.reshape(SEQS, SEQ_LEN, H)
```

```python
from contextlib import ExitStack

import concourse.bass as bass
from concourse import mybir

P = 128
F32 = mybir.dt.float32
F32R = mybir.dt.float32r
I32 = mybir.dt.int32
ALU = mybir.AluOpType
ACT = mybir.ActivationFunctionType

SEQS, SEQ_LEN, H, F, RANK = 8, 128, 512, 1376, 16
SLOTS0, SLOTS1 = 32, 16
TOKENS = SEQS * SEQ_LEN
HALF = TOKENS // 2
PAIRS = SEQS // 2
PAIR = 2 * SEQ_LEN
KT = H // P
FT = -(-F // P)
F_LAST = F - (FT - 1) * P
BLOCK = 4
BLOCKS = (FT - 1) // BLOCK
TAIL = FT - BLOCKS * BLOCK
BW = 2 * P

STAGE_A = KT // 2
STAGE_F = STAGE_A + 1
STAGE_BF = KT // 2
STAGE_BD = STAGE_BF + FT

C_MASK0, C_MASK1, C_SB, C_LB, C_ST, C_LT = 0, PAIR, 2 * PAIR, 2 * PAIR + 1, 2 * PAIR + 2, 2 * PAIR + 3
C_COLS = 2 * PAIR + 4

CREDIT = 2

WARM_UP = 12


def build(nc, xT, indices, w0T, bias, a0, b0, wgT, wuT, agu, bgu, wdT, ad, ad_last, bd, consts, outT):
    with ExitStack() as ctx:
        def sb(name, shape, dt=F32):
            return ctx.enter_context(nc.sbuf_tensor(name, shape, dt))

        def bank(name):
            return ctx.enter_context(nc.psum_tensor(name, [P, HALF], F32))

        def sem(name):
            return ctx.enter_context(nc.semaphore(name))

        b0_rows = nc.dram_tensor("b0_rows", (SEQS * RANK, H), F32, kind="Internal").ap()
        bgu_rows = nc.dram_tensor("bgu_rows", (SEQS * RANK, 2 * F), F32, kind="Internal").ap()
        bd_rows = nc.dram_tensor("bd_rows", (SEQS * RANK, H), F32, kind="Internal").ap()

        idx = sb("idx", [1, 2 * SEQS], I32)
        cst = sb("cst", [P, C_COLS])
        bias_sb = sb("bias_sb", [P, KT])
        x = sb("x", [P, KT, TOKENS])
        x1_hi = sb("x1_hi", [P, KT, TOKENS], F32R)
        x1_lo_sb = sb("x1_lo", [P, KT, TOKENS], F32R)
        act_hi = sb("act_hi", [P, BLOCK, TOKENS], F32R)
        act_lo = sb("act_lo", [P, BLOCK, TOKENS], F32R)
        raw_w = sb("raw_w", [P, 2, 2, KT, P])
        w_hi = sb("w_hi", [P, 2, 2, KT, P], F32R)
        w_lo = sb("w_lo", [P, 2, 2, KT, P], F32R)
        raw_agu = sb("raw_agu", [P, SEQS, 2, KT, RANK])
        raw_b = sb("raw_b", [P, 2, PAIRS, 2, P])
        b_x = sb("b_x", [P, 2, PAIRS, 2, P], F32R)
        raw_d = sb("raw_d", [P, 2, BLOCK, P])
        wd_hi = sb("wd_hi", [P, 2, BLOCK, P], F32R)
        wd_lo = sb("wd_lo", [P, 2, BLOCK, P], F32R)
        raw_a = sb("raw_a", [P, SEQS, BLOCK, RANK])
        a_x = sb("a_x", [P, BLOCK, 2, 2, 4 * RANK], F32R)
        t_low = sb("t_low", [P, PAIR])
        t_sum = sb("t_sum", [P, PAIR])
        t_gu = sb("t_gu", [P, PAIR])
        zeros = sb("zeros", [P, HALF], F32R)
        t_rep = sb("t_rep", [P, 2, 2, PAIR])
        t_x = sb("t_x", [P, PAIRS, PAIR], F32R)
        tgu_x = sb("tgu_x", [P, PAIRS, 2, PAIR], F32R)
        sil = sb("sil", [P, 2, HALF])
        act = sb("act", [P, 2, HALF])

        t_bank = [bank("t_bank0"), bank("t_bank1")]
        d_bank = [bank("d_bank0"), bank("d_bank1")]
        gu_bank = [[bank(f"gu_bank{h}{o}") for o in range(2)] for h in range(2)]
        wide = [gu_bank[0][0], gu_bank[0][1], gu_bank[1][0], gu_bank[1][1]]
        l0_bank = wide + [d_bank[0], d_bank[1], t_bank[0], t_bank[1]]
        tail_bank = [d_bank[0], d_bank[1]] + wide + [d_bank[0], d_bank[1]]

        idx_in, cst_in = sem("idx_in"), sem("cst_in")
        x_in = [sem(f"x_in{k}") for k in range(KT)]
        x_in_late = sem("x_in_late")
        w_in = [[sem(f"w_in{s}{o}") for o in range(2)] for s in range(2)]
        agu_in, a0_in, ad_in = sem("agu_in"), sem("a0_in"), sem("ad_in")
        b0_gathered, bgu_gathered, bd_gathered = sem("b0_gathered"), sem("bgu_gathered"), sem("bd_gathered")
        b_in = [sem("b_in0"), sem("b_in1")]
        d_in = [sem("d_in0"), sem("d_in1")]
        w_hi_ok, w_ok, w_free = sem("w_hi_ok"), sem("w_ok"), sem("w_free")
        w0_hi_ok, w0_ok = sem("w0_hi_ok"), sem("w0_ok")
        agu_hi_ok, agu_ok = sem("agu_hi_ok"), sem("agu_ok")
        f_hi_ok, f_ok = sem("f_hi_ok"), sem("f_ok")
        b_hi_ok, b_ok = sem("b_hi_ok"), sem("b_ok")
        d_hi_ok, d_ok, d_free = sem("d_hi_ok"), sem("d_ok"), sem("d_free")
        a_hi_ok, a_ok, a_free = sem("a_hi_ok"), sem("a_ok"), sem("a_free")
        x_hi_ok, x_lo_dve, x_lo_pool = sem("x_hi_ok"), sem("x_lo_dve"), sem("x_lo_pool")
        t_psum_ok, t_step, t_rep_ok, t_hi_ok, t_ok = (
            sem("t_psum_ok"), sem("t_step"), sem("t_rep_ok"), sem("t_hi_ok"), sem("t_ok"))
        l0_ok, x1_ok, x1_hi_ok = sem("l0_ok"), sem("x1_ok"), sem("x1_hi_ok")
        x1_lo_dve, x1_lo_pool = sem("x1_lo_dve"), sem("x1_lo_pool")
        gate_ok, up_ok, silu_ok, act_ok = sem("gate_ok"), sem("up_ok"), sem("silu_ok"), sem("act_ok")
        act_hi_ok, act_lo_ok = sem("act_hi_ok"), sem("act_lo_ok")
        down_ok, added = sem("down_ok"), sem("added")
        zeros_ok, out_done = sem("zeros_ok"), sem("out_done")

        def cols(h):
            return slice(h * HALF, (h + 1) * HALF)

        def f32(ap):
            return ap.bitcast(F32)

        def w_in_count(s):
            return 16 * (s // 2 + 1 - (1 if s % 2 == STAGE_A % 2 else 0)) if s > STAGE_A else 16

        def f_in_count(b, j):
            return b * (16 * BLOCK // 2) + w_in_count(STAGE_F + j)

        def b_in_count(b, j):
            return b * (64 * BLOCK // 2) + 64 * ((STAGE_BF + j) // 2 + 1)

        def w_slot(j):
            return (STAGE_F + j) % 2

        def b_slot(j):
            return (STAGE_BF + j) % 2

        def agu_views(w, s):
            half, a, e = s // 4, s % 4 // 2, s % 2
            to = w[:, STAGE_A % 2, half, :, 64 * a:64 * a + 64].rearrange("p k (o e r) -> p k o e r", o=2, e=2)
            return to[:, :, :, e, :], raw_agu[:, s].rearrange("p o k r -> p k o r")

        def slots(engine, first, count):
            _, values = nc.values_load_multi_w_load_instructions(
                idx[0:1, first:first + SEQS], engines=(engine,), min_val=0, max_val=count - 1)
            return values

        def a_part(h, part):
            return a_x[:, :, h, part, :].rearrange("p k (s r) -> p k s r", s=SEQS // 2)

        def a_whole(h):
            return raw_a[:, h * SEQS // 2:(h + 1) * SEQS // 2].rearrange("p s k r -> p k s r")

        block = ctx.enter_context(nc.Block())

        @block.sync
        def _(sp):
            def load_x(k):
                sp.dma_start(x[:, k, cols(0)], xT[0, :, k]).then_inc(x_in[k], 16)

            def load_w0(s, outs=(0, 1)):
                for o in outs:
                    sp.dma_start(raw_w[:, s, o, :, :], w0T[2 * s + o]).then_inc(w_in[s][o], 16)

            def load_b(slot, rows, c0, width, done):
                for q in range(4):
                    src = rows[:, bass.ds(c0, width)].rearrange("(a p) f -> p a f", a=PAIRS)
                    dst = raw_b[32 * q:32 * q + 32, slot, :, :, :].rearrange("p a o f -> p a (o f)")
                    sp.dma_start(dst[:, :, 0:width], src).then_inc(done, 16)

            load_w0(0, (0,))
            load_x(1)
            load_x(3)
            load_w0(0, (1,))
            load_w0(1)
            sp.dma_start(x[:, :, cols(1)], xT[1]).then_inc(x_in_late, 16)
            sp.wait_ge(idx_in, 16)
            slot0 = slots(mybir.EngineType.SP, 0, SLOTS0)
            for s in range(SEQS):
                sp.dma_start(raw_a[:, s, :, :],
                             a0[bass.ds(slot0[s], 1)].rearrange("a p k r -> (a p) k r")).then_inc(a0_in, 16)
            sp.dma_start(cst[:, :], consts).then_inc(cst_in, 16)
            sp.dma_start(bias_sb[:, :], bias).then_inc(cst_in, 16)
            for s in range(SEQS):
                sp.dma_start(b0_rows[s * RANK:(s + 1) * RANK, :],
                             b0[bass.ds(slot0[s], 1)].rearrange("a r f -> (a r) f")).then_inc(b0_gathered, 16)
            slot1 = slots(mybir.EngineType.SP, SEQS, SLOTS1)
            sp.wait_ge(b0_gathered, 16 * SEQS)
            load_b(0, b0_rows, 0, BW, b_in[0])
            load_b(1, b0_rows, BW, BW, b_in[1])
            for s in range(SEQS):
                sp.dma_start(bgu_rows[s * RANK:(s + 1) * RANK, :],
                             bgu[bass.ds(slot1[s], 1)].rearrange("a r f -> (a r) f")).then_inc(bgu_gathered, 16)

            def load_f_w(b, j, width=P):
                t = b * BLOCK + j
                if j >= 2:
                    sp.wait_ge(f_ok, t - 1)
                else:
                    sp.wait_ge(w_ok, STAGE_A - j)
                for o, w in ((0, wgT), (1, wuT)):
                    src = w[:, bass.ds(t * P, width)].rearrange("(k p) f -> p k f", p=P)
                    sp.dma_start(raw_w[:, w_slot(j), o, :, 0:width], src).then_inc(w_in[w_slot(j)][o], 16)

            def load_f_b(b, j):
                t = b * BLOCK + j
                sp.wait_ge(b_ok, t + (STAGE_BF - 1))
                load_b(b_slot(j), bgu_rows, t * BW, BW, b_in[b_slot(j)])

            def load_last_f_b(t):
                slot = b_slot(t)
                sp.wait_ge(b_ok, t + (STAGE_BF - 1))
                for q in range(4):
                    for o in range(2):
                        src = bgu_rows[:, t * BW + o * F_LAST:t * BW + (o + 1) * F_LAST]
                        sp.dma_start(raw_b[32 * q:32 * q + 32, slot, :, o, 0:F_LAST],
                                     src.rearrange("(a p) f -> p a f", a=PAIRS)).then_inc(b_in[slot], 16)

            def load_down_a(b, tiles):
                tail = isinstance(b, int)
                whole = tiles - 1 if tail else tiles
                sp.wait_ge(a_ok, b + 1)
                for s in range(SEQS):
                    src = ad[bass.ds(slot1[s], 1), :, bass.ds(b * BLOCK, whole), :]
                    sp.dma_start(raw_a[:, s, 0:whole, :], src.rearrange("a p k r -> (a p) k r")).then_inc(ad_in, 16)
                    if tail:
                        src = ad_last[bass.ds(slot1[s], 1)].rearrange("a p r -> (a p) r")
                        sp.dma_start(raw_a[0:F_LAST, s, whole, :], src).then_inc(ad_in, 16)

            def load_down_w(b, ht, tiles):
                whole = tiles - 1 if isinstance(b, int) else tiles
                sp.wait_ge(d_ok, b * KT + (ht + 1))
                src = wdT[bass.ds(b * (BLOCK * P), whole * P), ht * P:(ht + 1) * P]
                sp.dma_start(raw_d[:, ht % 2, 0:whole, :],
                             src.rearrange("(k p) f -> p k f", p=P)).then_inc(d_in[ht % 2], 16)
                if whole < tiles:
                    sp.dma_start(raw_d[0:F_LAST, ht % 2, whole, :],
                                 wdT[F - F_LAST:F, ht * P:(ht + 1) * P]).then_inc(d_in[ht % 2], 16)

            load_f_w(0, 0)
            sp.wait_ge(bgu_gathered, 16 * SEQS)
            load_f_b(0, 0)
            load_f_w(0, 1)
            load_f_b(0, 1)
            for s in range(SEQS):
                sp.dma_start(bd_rows[s * RANK:(s + 1) * RANK, :],
                             bd[bass.ds(slot1[s], 1)].rearrange("a r f -> (a r) f")).then_inc(bd_gathered, 16)
            with sp.Fori(0, BLOCKS) as b:
                load_f_w(b, 2)
                load_f_b(b, 2)
                load_f_w(b, 3)
                load_f_b(b, 3)
                load_down_a(b, BLOCK)
                load_down_w(b, 0, BLOCK)
                load_down_w(b, 1, BLOCK)
                load_f_w(b, 4)
                load_f_b(b, 4)
                load_down_w(b, 2, BLOCK)
                load_down_w(b, 3, BLOCK)
                load_f_w(b, 5)
                load_f_b(b, 5)
            load_f_w(BLOCKS, 2, F_LAST)
            load_last_f_b(FT - 1)
            load_down_a(BLOCKS, TAIL)
            for ht in range(2):
                load_down_w(BLOCKS, ht, TAIL)
            sp.wait_ge(bd_gathered, 16 * SEQS)
            for o in range(KT // 2):
                sp.wait_ge(b_ok, STAGE_BD + o - 1)
                load_b((STAGE_BD + o) % 2, bd_rows, o * BW, BW, b_in[(STAGE_BD + o) % 2])
                load_down_w(BLOCKS, 2 + o, TAIL)
            for ht in range(KT):
                for h in range(2):
                    sp.wait_ge(added, CREDIT + BLOCKS * 2 * KT + 2 * ht + h + 1)
                    sp.dma_start(outT[ht, :, cols(h)], x[:, ht, cols(h)]).then_inc(out_done, 16)
            sp.wait_ge(out_done, 16 * 2 * KT)

        @block.scalar
        def _(eng):
            eng.sem_inc(silu_ok, CREDIT)
            eng.dma_start(x[:, 0, cols(0)], xT[0, :, 0]).then_inc(x_in[0], 16)
            eng.dma_start(idx[:, :], indices).then_inc(idx_in, 16)
            eng.dma_start(x[:, 2, cols(0)], xT[0, :, 2]).then_inc(x_in[2], 16)
            eng.wait_ge(zeros_ok, 1)
            eng.activation(act[0:1, 0, 0:2], f32(zeros[0:1, 0:2]), ACT.Silu)

            def round_to(out, in_, scale=1.0):
                return eng.activation(out, in_, ACT.Copy, scale=scale)

            def x_hi(h, k):
                eng.wait_ge(x_in_late if h else x_in[k], 16)
                round_to(act_hi[:, k, cols(h)], x[:, k, cols(h)]).then_inc(x_hi_ok, 1)

            def b_hi_part(slot):
                round_to(b_x[:, slot], raw_b[:, slot], cst[:, C_SB:C_SB + 1]).then_inc(b_hi_ok, 1)

            def a_hi_part():
                for h in range(2):
                    last = round_to(a_part(h, 0), a_whole(h))
                last.then_inc(a_hi_ok, 1)

            def t_hi_part(n, out, in_):
                eng.wait_ge(t_rep_ok, n)
                round_to(out, in_, cst[:, C_ST:C_ST + 1]).then_inc(t_hi_ok, 1)

            def x1_hi_part(h, ot):
                eng.wait_ge(x1_ok, h * KT + ot + 1)
                round_to(x1_hi[:, ot, cols(h)], x[:, ot, cols(h)]).then_inc(x1_hi_ok, 1)

            eng.wait_ge(w_in[0][0], 16)
            round_to(w_hi[:, 0, 0], raw_w[:, 0, 0]).then_inc(w0_hi_ok, 1)
            for k in range(KT):
                x_hi(0, k)
            eng.wait_ge(w_in[0][1], 16)
            round_to(w_hi[:, 0, 1], raw_w[:, 0, 1]).then_inc(w_hi_ok, 1)
            eng.wait_ge(w_in[1][0], 16)
            eng.wait_ge(w_in[1][1], 16)
            round_to(w_hi[:, 1], raw_w[:, 1]).then_inc(w_hi_ok, 1)
            for k in range(KT):
                x_hi(1, k)
            eng.wait_ge(a0_in, 16 * SEQS)
            a_hi_part()
            eng.wait_ge(cst_in, 32)
            t_hi_part(1, t_x[:, 0:2, :], t_rep[:, 0])
            for s in range(2):
                eng.wait_ge(b_in[s], 64)
                b_hi_part(s)
            t_hi_part(2, t_x[:, 2:4, :], t_rep[:, 1])
            eng.wait_ge(agu_in, 16 * SEQS)
            eng.wait_ge(w_free, 1)
            for s in range(SEQS):
                dst, src = agu_views(w_hi, s)
                last = round_to(dst, src)
            last.then_inc(agu_hi_ok, 1)
            for h in range(2):
                for ot in range(KT):
                    x1_hi_part(h, ot)

            def f_hi(b, j, more=0):
                for o in range(2):
                    eng.wait_ge(w_in[w_slot(j)][o], f_in_count(b, j))
                if j == 1:
                    eng.wait_ge(t_psum_ok, 4)
                else:
                    eng.wait_ge(w_free, b * BLOCK + (STAGE_A + max(j - 1, 0)))
                round_to(w_hi[:, w_slot(j)], raw_w[:, w_slot(j)]).then_inc(f_hi_ok, 1)
                b_f_hi(b, j, more)

            def b_f_hi(b, j, more=0):
                eng.wait_ge(b_in[b_slot(j)], b_in_count(b, j) + more)
                if j >= 2:
                    eng.wait_ge(up_ok, b * (2 * BLOCK) + 2 * j)
                b_hi_part(b_slot(j))

            def a_d_hi(b, landed):
                eng.wait_ge(ad_in, landed)
                eng.wait_ge(a_free, b + 1)
                a_hi_part()

            def d_hi_part(b, ht, landed):
                eng.wait_ge(d_in[ht % 2], landed)
                if ht >= 2 and isinstance(b, int):
                    eng.wait_ge(d_free, ht - 1)
                elif ht >= 2:
                    eng.wait_ge(down_ok, b * (2 * KT) + (2 * ht - 2))
                round_to(wd_hi[:, ht % 2], raw_d[:, ht % 2]).then_inc(d_hi_ok, 1)

            def gate_tile(b, j, rows):
                for h in range(2):
                    n = 2 * (b * BLOCK + j) + h
                    eng.wait_ge(gate_ok, n + 1)
                    eng.wait_ge(act_ok, n + 1)
                    eng.activation(sil[0:rows, h], gu_bank[h][0][0:rows], ACT.Silu).then_inc(silu_ok, 1)
                    eng.wait_ge(act_ok, CREDIT + n + 1)
                    round_to(act_hi[0:rows, j, cols(h)], act[0:rows, h]).then_inc(act_hi_ok, 1)

            f_hi(0, 0)
            for h in range(2):
                t_hi_part(3 + h, tgu_x[:, 2 * h:2 * h + 2, :, :],
                          t_rep[:, :, :, :].rearrange("p o a t -> p a o t"))
                if h == 0:
                    f_hi(0, 1)

            with eng.Fori(0, BLOCKS) as b:
                gate_tile(b, 0, P)
                f_hi(b, 2)
                gate_tile(b, 1, P)
                f_hi(b, 3)
                a_d_hi(b, 16 * SEQS * (b + 1))
                gate_tile(b, 2, P)
                f_hi(b, 4)
                for ht in range(2):
                    d_hi_part(b, ht, 32 * b + 16)
                gate_tile(b, 3, P)
                f_hi(b, 5)
                for ht in range(2, KT):
                    d_hi_part(b, ht, 32 * b + 32)
            extra = [64 if (STAGE_BD + o) % 2 == b_slot(TAIL - 1) else 0 for o in range(2)]
            gate_tile(BLOCKS, 0, P)
            f_hi(BLOCKS, 2, 64)
            a_d_hi(BLOCKS, 16 * SEQS * (BLOCKS + 2))
            d_hi_part(BLOCKS, 0, 32 * BLOCKS + 32)
            gate_tile(BLOCKS, 1, P)
            d_hi_part(BLOCKS, 1, 32 * BLOCKS + 32)
            b_f_hi(BLOCKS, TAIL, extra[0])
            gate_tile(BLOCKS, 2, F_LAST)
            b_f_hi(BLOCKS, TAIL + 1, extra[1])
            t_hi_part(5, t_x[:, 0:2, :], t_rep[:, 0])
            d_hi_part(BLOCKS, 2, 32 * BLOCKS + 64)
            t_hi_part(6, t_x[:, 2:4, :], t_rep[:, 1])
            d_hi_part(BLOCKS, 3, 32 * BLOCKS + 64)

        @block.vector
        def _(eng):
            eng.sem_inc(act_ok, CREDIT)
            eng.sem_inc(d_ok, CREDIT)
            eng.sem_inc(added, CREDIT)

            def minus(out, whole, hi):
                return eng.tensor_tensor(out, whole, f32(hi), ALU.subtract)

            def x_lo(h, k):
                eng.wait_ge(x_hi_ok, h * KT + k + 1)
                minus(act_lo[:, k, cols(h)], x[:, k, cols(h)], act_hi[:, k, cols(h)]).then_inc(x_lo_dve, 1)

            def b_lo_part(n, slot):
                eng.wait_ge(b_hi_ok, n)
                eng.scalar_tensor_tensor(out=b_x[:, slot].rearrange("p a o f -> p (a o f)"),
                                         in0=raw_b[:, slot].rearrange("p a o f -> p (a o f)"),
                                         scalar=cst[:, C_LB:C_LB + 1],
                                         in1=f32(b_x[:, slot].rearrange("p a o f -> p (a o f)")),
                                         op0=ALU.mult, op1=ALU.add).then_inc(b_ok, 1)

            def a_lo_part(n):
                eng.wait_ge(a_hi_ok, n)
                for h in range(2):
                    last = minus(a_part(h, 1), a_whole(h), a_part(h, 0))
                last.then_inc(a_ok, 1)

            steps = [0]

            def step(op):
                op.then_inc(t_step, 1)
                steps[0] += 1

            def all_steps():
                eng.wait_ge(t_step, steps[0])

            def t_summed(n, h, mask):
                eng.wait_ge(t_psum_ok, n)
                ps = t_bank[h]
                for a in range(2):
                    row, col = slice(32 * a, 32 * a + 32), slice(a * PAIR, (a + 1) * PAIR)
                    step(eng.tensor_copy(t_low[row, :], ps[64 + 32 * a:96 + 32 * a, col]))
                all_steps()
                for a in range(2):
                    row, col = slice(32 * a, 32 * a + 32), slice(a * PAIR, (a + 1) * PAIR)
                    step(eng.tensor_tensor(t_sum[row, :], ps[row, col], t_low[row, :], ALU.add))
                all_steps()
                for a in range(2):
                    row = slice(32 * a, 32 * a + 32)
                    for q in range(4):
                        last = eng.tensor_tensor(t_rep[32 * q:32 * q + 32, h, a, :], t_sum[row, :],
                                                 cst[row, mask:mask + PAIR], ALU.mult)
                last.then_inc(t_rep_ok, 1)

            def t_gate_up(n, h):
                eng.wait_ge(t_psum_ok, n)
                for a in range(2):
                    col = slice(a * PAIR, (a + 1) * PAIR)
                    row = slice(64 * a, 64 * a + 64)
                    step(eng.tensor_tensor(t_gu[row, :], d_bank[h][row, col], cst[row, C_MASK1:C_MASK1 + PAIR],
                                           ALU.mult))
                all_steps()
                for a in range(2):
                    for o in range(2):
                        from_row = slice(64 * a + 32 * o, 64 * a + 32 * o + 32)
                        for q in range(4):
                            last = eng.tensor_copy(t_rep[32 * q:32 * q + 32, o, a, :], t_gu[from_row, :])
                last.then_inc(t_rep_ok, 1)

            def t_lo_part(n, out, in_):
                eng.wait_ge(t_hi_ok, n)
                eng.scalar_tensor_tensor(out=out, in0=in_, scalar=cst[:, C_LT:C_LT + 1], in1=f32(out),
                                         op0=ALU.mult, op1=ALU.add).then_inc(t_ok, 1)

            def t_lo_of_half(n, h):
                t_lo_part(n, t_x[:, 2 * h:2 * h + 2, :].rearrange("p a t -> p (a t)"),
                          t_rep[:, h].rearrange("p a t -> p (a t)"))

            def x1_part(h, ot):
                eng.wait_ge(l0_ok, h * KT + ot + 1)
                eng.scalar_tensor_tensor(out=x[:, ot, cols(h)], in0=l0_bank[h * KT + ot][:, :],
                                         scalar=bias_sb[:, ot:ot + 1], in1=x[:, ot, cols(h)],
                                         op0=ALU.add, op1=ALU.add).then_inc(x1_ok, 1)

            eng.wait_ge(w0_hi_ok, 1)
            minus(w_lo[:, 0, 0], raw_w[:, 0, 0], w_hi[:, 0, 0]).then_inc(w0_ok, 1)
            x_lo(0, 0)
            x_lo(0, 2)
            eng.wait_ge(w_hi_ok, 1)
            minus(w_lo[:, 0, 1], raw_w[:, 0, 1], w_hi[:, 0, 1]).then_inc(w_ok, 1)
            eng.wait_ge(w_hi_ok, 2)
            minus(w_lo[:, 1], raw_w[:, 1], w_hi[:, 1]).then_inc(w_ok, 1)
            x_lo(1, 1)
            x_lo(1, 3)
            a_lo_part(1)
            eng.wait_ge(cst_in, 32)
            for h in range(2):
                t_summed(h + 1, h, C_MASK0)
            t_lo_of_half(1, 0)
            b_lo_part(1, 0)
            b_lo_part(2, 1)
            t_lo_of_half(2, 1)

            def x1_lo(h, ot):
                eng.wait_ge(x1_hi_ok, h * KT + ot + 1)
                minus(x1_lo_sb[:, ot, cols(h)], x[:, ot, cols(h)], x1_hi[:, ot, cols(h)]).then_inc(x1_lo_dve, 1)

            for h in range(2):
                for ot in range(KT):
                    x1_part(h, ot)
                    if ot == 2:
                        x1_lo(h, 1)
                x1_lo(h, 3)

            def b_f_lo(b, j):
                b_lo_part(b * BLOCK + (STAGE_BF + j + 1), b_slot(j))

            def d_lo_part(b, ht):
                eng.wait_ge(d_hi_ok, b * KT + (ht + 1))
                minus(wd_lo[:, ht % 2], raw_d[:, ht % 2], wd_hi[:, ht % 2]).then_inc(d_ok, 1)

            def up_tile(b, j, rows):
                for h in range(2):
                    n = 2 * (b * BLOCK + j) + h
                    eng.wait_ge(up_ok, CREDIT + n + 1)
                    eng.wait_ge(silu_ok, CREDIT + n + 1)
                    eng.wait_ge(act_lo_ok, n + 1)
                    eng.tensor_tensor(act[0:rows, h], gu_bank[h][1][0:rows], sil[0:rows, h],
                                      ALU.mult).then_inc(act_ok, 1)

            def add_down(b, ht, banks):
                for h in range(2):
                    eng.wait_ge(down_ok, b * (2 * KT) + (2 * ht + h + 1))
                    eng.tensor_tensor(x[:, ht, cols(h)], banks[h][:, :], x[:, ht, cols(h)],
                                      ALU.add).then_inc(added, 1)

            b_f_lo(0, 0)
            for h in range(2):
                t_gate_up(3 + h, h)
                eng.wait_ge(t_hi_ok, 3 + h)
                for a in range(2):
                    last = eng.scalar_tensor_tensor(
                        out=tgu_x[:, 2 * h + a, :, :], in0=t_rep[:, :, a, :], scalar=cst[:, C_LT:C_LT + 1],
                        in1=f32(tgu_x[:, 2 * h + a, :, :]), op0=ALU.mult, op1=ALU.add)
                last.then_inc(t_ok, 1)
            b_f_lo(0, 1)

            with eng.Fori(0, BLOCKS) as b:
                up_tile(b, 0, P)
                b_f_lo(b, 2)
                up_tile(b, 1, P)
                b_f_lo(b, 3)
                a_lo_part(b + 2)
                up_tile(b, 2, P)
                b_f_lo(b, 4)
                d_lo_part(b, 0)
                d_lo_part(b, 1)
                up_tile(b, 3, P)
                b_f_lo(b, 5)
                for ht in range(KT):
                    add_down(b, ht, d_bank)
                    if ht + 2 < KT:
                        d_lo_part(b, ht + 2)
            up_tile(BLOCKS, 0, P)
            b_f_lo(BLOCKS, 2)
            a_lo_part(BLOCKS + 2)
            d_lo_part(BLOCKS, 0)
            up_tile(BLOCKS, 1, P)
            d_lo_part(BLOCKS, 1)
            b_f_lo(BLOCKS, TAIL)
            up_tile(BLOCKS, 2, F_LAST)
            for h in range(2):
                t_summed(5 + h, h, C_MASK1)
            t_lo_of_half(5, 0)
            t_lo_of_half(6, 1)
            b_f_lo(BLOCKS, TAIL + 1)
            for ht in range(KT):
                add_down(BLOCKS, ht, tail_bank[2 * ht:2 * ht + 2])

        @block.gpsimd
        def _(eng):
            eng.sem_inc(act_lo_ok, CREDIT)
            eng.memset(f32(zeros[:, :]), 0.0).then_inc(zeros_ok, 1)

            def minus(out, whole, hi):
                return eng.tensor_tensor(out, whole, f32(hi), ALU.subtract)

            for h, k in ((0, 1), (0, 3), (1, 0), (1, 2)):
                eng.wait_ge(x_hi_ok, h * KT + k + 1)
                minus(act_lo[:, k, cols(h)], x[:, k, cols(h)], act_hi[:, k, cols(h)]).then_inc(x_lo_pool, 1)
            eng.wait_ge(idx_in, 16)
            slot1 = slots(mybir.EngineType.Pool, SEQS, SLOTS1)
            for s in range(SEQS):
                eng.dma_start(raw_agu[:, s, :, :, :], agu[bass.ds(slot1[s], 1)].rearrange(
                    "a p o k r -> (a p) o k r")).then_inc(agu_in, 16)
            eng.wait_ge(agu_hi_ok, 1)
            for s in range(SEQS):
                hi, src = agu_views(w_hi, s)
                dst, _ = agu_views(w_lo, s)
                last = minus(dst, src, hi)
            last.then_inc(agu_ok, 1)
            for h in range(2):
                for ot in (0, 2):
                    eng.wait_ge(x1_hi_ok, h * KT + ot + 1)
                    minus(x1_lo_sb[:, ot, cols(h)], x[:, ot, cols(h)],
                          x1_hi[:, ot, cols(h)]).then_inc(x1_lo_pool, 1)

            def f_lo(b, j):
                eng.wait_ge(f_hi_ok, b * BLOCK + (j + 1))
                minus(w_lo[:, w_slot(j)], raw_w[:, w_slot(j)], w_hi[:, w_slot(j)]).then_inc(f_ok, 1)

            def act_lo_tile(b, j, rows):
                for h in range(2):
                    eng.wait_ge(act_hi_ok, 2 * (b * BLOCK + j) + h + 1)
                    minus(act_lo[0:rows, j, cols(h)], act[0:rows, h],
                          act_hi[0:rows, j, cols(h)]).then_inc(act_lo_ok, 1)

            f_lo(0, 0)
            f_lo(0, 1)
            with eng.Fori(0, BLOCKS) as b:
                for j in range(BLOCK):
                    act_lo_tile(b, j, P)
                    f_lo(b, j + 2)
            act_lo_tile(BLOCKS, 0, P)
            f_lo(BLOCKS, 2)
            act_lo_tile(BLOCKS, 1, P)
            act_lo_tile(BLOCKS, 2, F_LAST)
            for ht in range(2, KT):
                eng.wait_ge(d_hi_ok, BLOCKS * KT + ht + 1)
                minus(wd_lo[:, ht % 2], raw_d[:, ht % 2], wd_hi[:, ht % 2]).then_inc(d_ok, 1)

        @block.tensor
        def _(eng):
            eng.sem_inc(up_ok, CREDIT)

            def split_product(out, hi, lo, in_hi, in_lo, start, stop=False):
                eng.matmul(out, hi, in_hi, start=start, stop=False)
                eng.matmul(out, hi, in_lo, start=False, stop=False)
                return eng.matmul(out, lo, in_hi, start=False, stop=stop)

            def wide_sum(out, slot, o, in_hi, in_lo, h, stop=False):
                for k in range(KT):
                    last = split_product(out, w_hi[:, slot, o, k, :], w_lo[:, slot, o, k, :],
                                         in_hi[:, k, cols(h)], in_lo[:, k, cols(h)], k == 0,
                                         stop and k == KT - 1)
                return last

            def lora(out, slot, o, t, h):
                for a in range(2):
                    last = eng.matmul(out[:, a * PAIR:(a + 1) * PAIR], b_x[:, slot, 2 * h + a, o, :],
                                      t[:, 2 * h + a, :], start=False, stop=a == 1)
                return last

            def l0_main(h, ot):
                return wide_sum(l0_bank[h * KT + ot][:, :], ot // 2, ot % 2, act_hi, act_lo, h)

            def project(out, h, n_k, start, first, k_rows=P, stop=True):
                for k in range(n_k):
                    if first is not None:
                        eng.wait_ge(act_lo_ok, first + 2 * k)
                    rows = slice(0, k_rows if k == n_k - 1 else P)
                    for v in (act_hi, act_lo):
                        last = eng.matmul(out, a_x[rows, k, h, :, :].rearrange("p v c -> p (v c)"),
                                          v[rows, k, cols(h)], start=start and k == 0 and v is act_hi,
                                          stop=stop and k == n_k - 1 and v is act_lo)
                return last

            def l0_lora(h, ot):
                return lora(l0_bank[h * KT + ot], ot // 2, ot % 2, t_x, h).then_inc(l0_ok, 1)

            eng.wait_ge(zeros_ok, 1)
            for _ in range(WARM_UP):
                eng.matmul(d_bank[0][:, :], zeros[:, 0:P], zeros[:, :], start=True, stop=True)
            eng.wait_ge(w0_ok, 1)
            for k in range(KT):
                if k % 2 == 0:
                    eng.wait_ge(x_lo_dve, k // 2 + 1)
                else:
                    eng.wait_ge(x_lo_pool, k // 2 + 1)
                split_product(l0_bank[0][:, :], w_hi[:, 0, 0, k, :], w_lo[:, 0, 0, k, :],
                              act_hi[:, k, cols(0)], act_lo[:, k, cols(0)], k == 0)
            eng.wait_ge(w_ok, 1)
            l0_main(0, 1)
            eng.wait_ge(w_ok, 2)
            l0_main(0, 2)
            eng.wait_ge(a_ok, 1)
            project(t_bank[0][:, :], 0, KT, True, None).then_inc(t_psum_ok, 1)
            eng.wait_ge(x_lo_pool, KT)
            eng.wait_ge(x_lo_dve, KT)
            project(t_bank[1][:, :], 1, KT, True, None).then_inc(t_psum_ok, 1)
            eng.sem_inc(a_free, 1)
            l0_main(0, 3)
            l0_main(1, 0)
            l0_main(1, 1).then_inc(w_free, 1)
            eng.wait_ge(t_ok, 1)
            eng.wait_ge(b_ok, 2)
            for ot in range(KT):
                l0_lora(0, ot)
            l0_main(1, 2)
            eng.wait_ge(t_ok, 2)
            for ot in range(KT - 1):
                l0_lora(1, ot)
            l0_main(1, 3).then_inc(w_free, 1)
            l0_lora(1, KT - 1)

            for h in range(2):
                eng.wait_ge(x1_ok, KT + h + 1)
                eng.wait_ge(x1_lo_dve, (h + 1) * KT // 2)
                eng.wait_ge(x1_lo_pool, (h + 1) * KT // 2)
                if h == 0:
                    eng.wait_ge(agu_ok, 1)
                last = wide_sum(d_bank[h][:, :], STAGE_A % 2, h, x1_hi, x1_lo_sb, h, stop=True)
                last.then_inc(t_psum_ok, 1)
            for h in range(2):
                eng.matmul(t_bank[h][:, :], zeros[:, 0:P], zeros[:, :], start=True, stop=False)

            def f_tile(b, j, last_tile=False):
                width = F_LAST if last_tile else P
                t = b * BLOCK + j
                ws, bs = w_slot(j), b_slot(j)
                eng.wait_ge(f_ok, t + 1)
                for h in range(2):
                    n = 2 * t + h
                    for o in range(2):
                        eng.wait_ge((silu_ok, act_ok)[o], n + 1)
                        for k in range(KT):
                            last = split_product(gu_bank[h][o][0:width, :], w_hi[:, ws, o, k, 0:width],
                                                 w_lo[:, ws, o, k, 0:width], x1_hi[:, k, cols(h)],
                                                 x1_lo_sb[:, k, cols(h)], k == 0)
                    if h == 1:
                        last.then_inc(w_free, 1)
                    else:
                        eng.wait_ge(b_ok, t + (STAGE_BF + 1))
                    eng.wait_ge(t_ok, 3 + h)
                    for o in range(2):
                        for a in range(2):
                            last = eng.matmul(gu_bank[h][o][0:width, a * PAIR:(a + 1) * PAIR],
                                              b_x[:, bs, 2 * h + a, o, 0:width], tgu_x[:, 2 * h + a, o, :],
                                              start=False, stop=a == 1)
                        last.then_inc((gate_ok, up_ok)[o], 1)

            def down_sum(out, ht, h, n_k, k_rows=P, stop=True):
                for k in range(n_k):
                    rows = slice(0, k_rows if k == n_k - 1 else P)
                    last = split_product(out, wd_hi[rows, ht % 2, k, :], wd_lo[rows, ht % 2, k, :],
                                         act_hi[rows, k, cols(h)], act_lo[rows, k, cols(h)], k == 0,
                                         stop and k == n_k - 1)
                return last

            with eng.Fori(0, BLOCKS) as b:
                for j in range(BLOCK):
                    f_tile(b, j)
                eng.wait_ge(a_ok, b + 2)
                for n in range(2 * KT):
                    ht, h = n // 2, n % 2
                    if ht == 0:
                        last = project(t_bank[h][:, :], h, BLOCK, False, b * (2 * BLOCK) + (CREDIT + h + 1),
                                       stop=False)
                        if h == 1:
                            last.then_inc(a_free, 1)
                    if h == 0:
                        eng.wait_ge(d_ok, b * KT + (CREDIT + ht + 1))
                    eng.wait_ge(added, b * (2 * KT) + (n + 1))
                    down_sum(d_bank[h][:, :], ht, h, BLOCK).then_inc(down_ok, 1)
            for j in range(TAIL):
                f_tile(BLOCKS, j, j == TAIL - 1)

            eng.wait_ge(a_ok, BLOCKS + 2)

            def down_main(n):
                ht, h = n // 2, n % 2
                eng.wait_ge(d_ok, BLOCKS * KT + CREDIT + ht + 1)
                if n < 2:
                    project(t_bank[h][:, :], h, TAIL, False, BLOCKS * 2 * BLOCK + CREDIT + h + 1,
                            F_LAST).then_inc(t_psum_ok, 1)
                    eng.wait_ge(added, BLOCKS * 2 * KT + n + 1)
                elif n >= 6:
                    eng.wait_ge(added, BLOCKS * 2 * KT + CREDIT + n - 5)
                last = down_sum(tail_bank[n][:, :], ht, h, TAIL, F_LAST, stop=False)
                if h == 1:
                    last.then_inc(d_free, 1)

            def down_lora(n):
                ht, h = n // 2, n % 2
                if n < 2:
                    eng.wait_ge(t_ok, 5 + n)
                eng.wait_ge(b_ok, STAGE_BD + ht // 2 + 1)
                lora(tail_bank[n], (STAGE_BD + ht // 2) % 2, ht % 2, t_x, h).then_inc(down_ok, 1)

            for n, loras in enumerate([(), (), (), (), (0,), (1, 2), (3, 4, 5, 6), (7,)]):
                down_main(n)
                for m in loras:
                    down_lora(m)


def kernel(x, itok_B_0_23, itok_B_2_6, L0_cond_W, L0_cond_b, L0_cond_lora_As, L0_cond_lora_Bs, L1_cond_W_gate,
           L1_cond_W_up, L1_cond_W_down, L1_cond_A_gate, L1_cond_B_gate, L1_cond_A_up, L1_cond_B_up,
           L1_cond_A_down, L1_cond_B_down):
    import numpy as np
    import concourse.bacc as bacc
    from concourse.bass_utils import run_bass_kernel_spmd

    def tiles(a):
        return a.reshape(a.shape[0], -1, P, a.shape[-1]).transpose(0, 2, 1, 3)

    p, t = np.arange(P), np.arange(PAIR)
    same = (p[:, None] % 32 // RANK == t[None, :] // SEQ_LEN).astype(np.float32)
    b_low, t_low = (p // 32 % 2).astype(np.float32), (p // 64).astype(np.float32)
    consts = np.concatenate([same * 2.0, same * 0.5, np.stack([1 - 2 * b_low, b_low, 1 - 2 * t_low, t_low], 1)],
                            axis=1).astype(np.float32)

    whole = (FT - 1) * P
    b_gate, b_up = (a[0].transpose(0, 2, 1) for a in (L1_cond_B_gate, L1_cond_B_up))
    b_gu = np.stack([b_gate[:, :, :whole].reshape(SLOTS1, RANK, FT - 1, P),
                     b_up[:, :, :whole].reshape(SLOTS1, RANK, FT - 1, P)], axis=3)
    b_last = np.stack([b_gate[:, :, whole:], b_up[:, :, whole:]], axis=2)
    arrays = {
        "xT": x.reshape(2, HALF, KT, P).transpose(0, 3, 2, 1),
        "indices": np.concatenate([itok_B_0_23, itok_B_2_6]).reshape(1, 2 * SEQS),
        "w0T": L0_cond_W.reshape(KT, P, KT, P).transpose(0, 3, 2, 1),
        "bias": L0_cond_b.reshape(KT, P).T,
        "a0": tiles(L0_cond_lora_As),
        "b0": L0_cond_lora_Bs,
        "wgT": L1_cond_W_gate.T,
        "wuT": L1_cond_W_up.T,
        "agu": np.stack([tiles(a[0].transpose(0, 2, 1)) for a in (L1_cond_A_gate, L1_cond_A_up)], axis=2),
        "bgu": np.concatenate([b_gu.reshape(SLOTS1, RANK, -1),
                               b_last.reshape(SLOTS1, RANK, -1)], axis=2),
        "wdT": L1_cond_W_down.T,
        "ad": tiles(L1_cond_A_down[0].transpose(0, 2, 1)[:, :whole]),
        "ad_last": L1_cond_A_down[0].transpose(0, 2, 1)[:, whole:],
        "bd": L1_cond_B_down[0].transpose(0, 2, 1),
        "consts": consts,
    }
    arrays = {name: np.ascontiguousarray(a) for name, a in arrays.items()}
    nc = bacc.Bacc("TRN2", target_bir_lowering=False, num_devices=1)
    ins = {name: nc.dram_tensor(name, a.shape, mybir.dt.from_np(a.dtype), kind="ExternalInput").ap()
           for name, a in arrays.items()}
    outT = nc.dram_tensor("outT", (KT, P, TOKENS), F32, kind="ExternalOutput").ap()
    build(nc, outT=outT, **ins)
    result = run_bass_kernel_spmd(nc, [arrays], core_ids=[0])
    return result.results[0]["outT"].reshape(H, TOKENS).T.reshape(SEQS, SEQ_LEN, H)
```

```python
from contextlib import ExitStack

import concourse.bass as bass
from concourse import mybir

P = 128
F32 = mybir.dt.float32
F32R = mybir.dt.float32r
I32 = mybir.dt.int32
ALU = mybir.AluOpType
ACT = mybir.ActivationFunctionType

SEQS, SEQ_LEN, H, F, RANK = 8, 128, 512, 1376, 16
SLOTS0, SLOTS1 = 32, 16
TOKENS = SEQS * SEQ_LEN
HALF = TOKENS // 2
PAIRS = SEQS // 2
PAIR = 2 * SEQ_LEN
KT = H // P
FT = -(-F // P)
F_LAST = F - (FT - 1) * P
BLOCK = 4
BLOCKS = (FT - 1) // BLOCK
TAIL = FT - BLOCKS * BLOCK
BW = 2 * P

STAGE_A = KT // 2
STAGE_F = STAGE_A + 1
STAGE_BF = KT // 2
STAGE_BD = STAGE_BF + FT

C_MASK0, C_MASK1, C_SB, C_LB, C_COLS = 0, PAIR, 2 * PAIR, 2 * PAIR + 1, 2 * PAIR + 2

CREDIT = 2

WARM_UP = 8


def build(nc, xT, indices, w0T, bias, a0, b0, wgT, wuT, agu, bgu, wdT, ad, ad_last, bd, consts, outT):
    with ExitStack() as ctx:
        def sb(name, shape, dt=F32):
            return ctx.enter_context(nc.sbuf_tensor(name, shape, dt))

        def bank(name):
            return ctx.enter_context(nc.psum_tensor(name, [P, HALF], F32))

        def sem(name):
            return ctx.enter_context(nc.semaphore(name))

        bgu_rows = nc.dram_tensor("bgu_rows", (SEQS * RANK, 2 * F), F32, kind="Internal").ap()
        bd_rows = nc.dram_tensor("bd_rows", (SEQS * RANK, H), F32, kind="Internal").ap()

        idx = sb("idx", [1, 2 * SEQS], I32)
        cst = sb("cst", [P, C_COLS])
        bias_sb = sb("bias_sb", [P, KT])
        x = sb("x", [P, KT, TOKENS])
        x1_hi = sb("x1_hi", [P, KT, TOKENS], F32R)
        x1_lo_sb = sb("x1_lo", [P, KT, TOKENS], F32R)
        act_hi = sb("act_hi", [P, BLOCK, TOKENS], F32R)
        act_lo = sb("act_lo", [P, BLOCK, TOKENS], F32R)
        raw_w = sb("raw_w", [P, 2, 2, KT, P])
        w_hi = sb("w_hi", [P, 2, 2, KT, P], F32R)
        w_lo = sb("w_lo", [P, 2, 2, KT, P], F32R)
        raw_agu = sb("raw_agu", [P, SEQS, 2, KT, RANK])
        raw_b = sb("raw_b", [P, 2, PAIRS, 2, P])
        b_x = sb("b_x", [P, 2, PAIRS, 2, P], F32R)
        raw_d = sb("raw_d", [P, 2, BLOCK, P])
        wd_hi = sb("wd_hi", [P, 2, BLOCK, P], F32R)
        wd_lo = sb("wd_lo", [P, 2, BLOCK, P], F32R)
        raw_a = sb("raw_a", [P, SEQS, BLOCK, RANK])
        a_x = sb("a_x", [P, BLOCK, 2, 2, 4 * RANK], F32R)
        t_low = sb("t_low", [2 * 32, 2, PAIR])
        t_sum = sb("t_sum", [2 * 32, 2, PAIR])
        t_whole = sb("t_whole", [P, 2, PAIR])
        t_hi = sb("t_hi", [P, 2, PAIR], F32R)
        zeros = sb("zeros", [P, HALF], F32R)
        t_x = sb("t_x", [P, PAIRS, PAIR], F32R)
        tgu_x = sb("tgu_x", [P, PAIRS, 2, PAIR], F32R)
        sil = sb("sil", [P, 2, HALF])
        act = sb("act", [P, 2, HALF])

        t_bank = [bank("t_bank0"), bank("t_bank1")]
        d_bank = [bank("d_bank0"), bank("d_bank1")]
        gu_bank = [[bank(f"gu_bank{h}{o}") for o in range(2)] for h in range(2)]
        wide = [gu_bank[0][0], gu_bank[0][1], gu_bank[1][0], gu_bank[1][1]]
        l0_bank = wide + [d_bank[0], d_bank[1], t_bank[0], t_bank[1]]
        tail_bank = [d_bank[0], d_bank[1]] + wide + [d_bank[0]]

        idx_in, cst_in = sem("idx_in"), sem("cst_in")
        bias_in, b0_in = sem("bias_in"), sem("b0_in")
        x_in = [sem(f"x_in{k}") for k in range(KT)]
        x_in_late = sem("x_in_late")
        w_in = [[sem(f"w_in{s}{o}") for o in range(2)] for s in range(2)]
        agu_in, a0_in, ad_in = sem("agu_in"), sem("a0_in"), sem("ad_in")
        b0_gathered, bgu_gathered, bd_gathered = sem("b0_gathered"), sem("bgu_gathered"), sem("bd_gathered")
        b_in = [sem("b_in0"), sem("b_in1")]
        d_in = [sem("d_in0"), sem("d_in1")]
        w_hi_ok, w_ok, w_free = sem("w_hi_ok"), sem("w_ok"), sem("w_free")
        w0_hi_ok, w0_ok = sem("w0_hi_ok"), sem("w0_ok")
        agu_hi_ok, agu_ok = sem("agu_hi_ok"), sem("agu_ok")
        f_hi_ok, f_ok = sem("f_hi_ok"), sem("f_ok")
        b_hi_ok, b_ok = sem("b_hi_ok"), sem("b_ok")
        d_hi_ok, d_ok, d_free = sem("d_hi_ok"), sem("d_ok"), sem("d_free")
        a_hi_ok, a_ok, a_free = sem("a_hi_ok"), sem("a_ok"), sem("a_free")
        x_hi_ok, x_lo_dve, x_lo_pool = sem("x_hi_ok"), sem("x_lo_dve"), sem("x_lo_pool")
        t_psum_ok, t_low_ok, t_sum_ok, t_whole_ok = (
            sem("t_psum_ok"), sem("t_low_ok"), sem("t_sum_ok"), sem("t_whole_ok"))
        t_round_ok, t_hi_ok, t_lo_ok = sem("t_round_ok"), sem("t_hi_ok"), sem("t_lo_ok")
        l0_ok, x1_ok, x1_hi_ok = sem("l0_ok"), sem("x1_ok"), sem("x1_hi_ok")
        x1_lo_dve, x1_lo_pool = sem("x1_lo_dve"), sem("x1_lo_pool")
        gate_ok, up_ok, silu_ok, act_ok = sem("gate_ok"), sem("up_ok"), sem("silu_ok"), sem("act_ok")
        act_hi_ok, act_lo_ok = sem("act_hi_ok"), sem("act_lo_ok")
        down_ok, added = sem("down_ok"), sem("added")
        zeros_ok, out_done = sem("zeros_ok"), sem("out_done")

        def cols(h):
            return slice(h * HALF, (h + 1) * HALF)

        out_parts = [(tail_bank[n], n // 2, n % 2, slice(0, HALF)) for n in range(2 * KT - 1)]
        out_parts += [(tail_bank[1 + a], KT - 1, 1, slice(a * PAIR, (a + 1) * PAIR)) for a in range(2)]

        def of_half(h, part):
            return slice(h * HALF + part.start, h * HALF + part.stop)

        def f32(ap):
            return ap.bitcast(F32)

        def f_in_count(b, j):
            s = STAGE_F + j
            return b * (16 * BLOCK // 2) + 16 * (s // 2 + 1 - (s % 2 == STAGE_A % 2))

        def b_in_count(b, j):
            return b * (64 * BLOCK // 2) + 64 * (j // 2 + 1)

        def t_places(out, rows, q0):
            return [(out[32 * q:32 * q + 32], rows) for q in (q0, q0 + 1)]

        def t_pairs(h, q0):
            return [place for a in range(2)
                    for place in t_places(t_x[:, 2 * h + a, :], slice(32 * a, 32 * a + 32), q0)]

        def tgu_pairs(h, q0):
            return [place for a in range(2) for o in range(2)
                    for place in t_places(tgu_x[:, 2 * h + a, o, :],
                                          slice(64 * a + 32 * o, 64 * a + 32 * o + 32), q0)]

        def w_slot(j):
            return (STAGE_F + j) % 2

        def b_slot(j):
            return (STAGE_BF + j) % 2

        def agu_views(w, s):
            half, a, e = s // 4, s % 4 // 2, s % 2
            to = w[:, STAGE_A % 2, half, :, 64 * a:64 * a + 64].rearrange("p k (o e r) -> p k o e r", o=2, e=2)
            return to[:, :, :, e, :], raw_agu[:, s].rearrange("p o k r -> p k o r")

        def slots(engine, first, count):
            _, values = nc.values_load_multi_w_load_instructions(
                idx[0:1, first:first + SEQS], engines=(engine,), min_val=0, max_val=count - 1)
            return values

        def a_part(h, part):
            return a_x[:, :, h, part, :].rearrange("p k (s r) -> p k s r", s=SEQS // 2)

        def a_whole(h):
            return raw_a[:, h * SEQS // 2:(h + 1) * SEQS // 2].rearrange("p s k r -> p k s r")

        block = ctx.enter_context(nc.Block())

        @block.sync
        def _(sp):
            def load_x(k):
                sp.dma_start(x[:, k, cols(0)], xT[0, :, k]).then_inc(x_in[k], 16)

            def load_w0(s, outs=(0, 1)):
                for o in outs:
                    sp.dma_start(raw_w[:, s, o, :, :], w0T[2 * s + o]).then_inc(w_in[s][o], 16)

            def load_b(slot, rows, c0, width, done):
                for q in range(4):
                    src = rows[:, bass.ds(c0, width)].rearrange("(a p) f -> p a f", a=PAIRS)
                    dst = raw_b[32 * q:32 * q + 32, slot, :, :, :].rearrange("p a o f -> p a (o f)")
                    sp.dma_start(dst[:, :, 0:width], src).then_inc(done, 16)

            load_w0(0, (0,))
            for k in range(1, KT):
                load_x(k)
            load_w0(0, (1,))
            load_w0(1)
            sp.dma_start(x[:, :, cols(1)], xT[1]).then_inc(x_in_late, 16)
            sp.wait_ge(idx_in, 16)
            slot0 = slots(mybir.EngineType.SP, 0, SLOTS0)
            for s in range(SEQS):
                sp.dma_start(raw_a[:, s, :, :],
                             a0[bass.ds(slot0[s], 1)].rearrange("a p k r -> (a p) k r")).then_inc(a0_in, 16)
            for s in range(SEQS):
                rows = slice(s % 2 * RANK, (s % 2 + 1) * RANK)
                sp.dma_start(raw_b[rows, :, s // 2, :, :],
                             b0[bass.ds(slot0[s], 1)].rearrange("a r (i o f) -> (a r) i o f", i=2, o=2)
                             ).then_inc(b0_gathered, 16)
            sp.dma_start(cst[:, :], consts).then_inc(cst_in, 16)
            slot1 = slots(mybir.EngineType.SP, SEQS, SLOTS1)
            sp.wait_ge(b0_gathered, 16 * SEQS)
            for q in range(1, 4):
                sp.dma_start(raw_b[32 * q:32 * q + 32], raw_b[0:32]).then_inc(b0_in, 16)
            sp.dma_start(bias_sb[:, :], bias).then_inc(bias_in, 16)
            for s in range(SEQS):
                sp.dma_start(bgu_rows[s * RANK:(s + 1) * RANK, :],
                             bgu[bass.ds(slot1[s], 1)].rearrange("a r f -> (a r) f")).then_inc(bgu_gathered, 16)

            def load_f_w(b, j, width=P):
                t = b * BLOCK + j
                if j >= 2:
                    sp.wait_ge(f_ok, t - 1)
                else:
                    sp.wait_ge(w_ok, STAGE_A - j)
                for o, w in ((0, wgT), (1, wuT)):
                    src = w[:, bass.ds(t * P, width)].rearrange("(k p) f -> p k f", p=P)
                    sp.dma_start(raw_w[:, w_slot(j), o, :, 0:width], src).then_inc(w_in[w_slot(j)][o], 16)

            def load_f_b(b, j):
                t = b * BLOCK + j
                sp.wait_ge(b_ok, t + (STAGE_BF - 1))
                load_b(b_slot(j), bgu_rows, t * BW, BW, b_in[b_slot(j)])

            def load_last_f_b(t):
                slot = b_slot(t)
                sp.wait_ge(b_ok, t + (STAGE_BF - 1))
                for q in range(4):
                    for o in range(2):
                        src = bgu_rows[:, t * BW + o * F_LAST:t * BW + (o + 1) * F_LAST]
                        sp.dma_start(raw_b[32 * q:32 * q + 32, slot, :, o, 0:F_LAST],
                                     src.rearrange("(a p) f -> p a f", a=PAIRS)).then_inc(b_in[slot], 16)

            def load_down_a(b, tiles):
                tail = isinstance(b, int)
                whole = tiles - 1 if tail else tiles
                sp.wait_ge(a_ok, b + 1)
                for s in range(SEQS):
                    src = ad[bass.ds(slot1[s], 1), :, bass.ds(b * BLOCK, whole), :]
                    sp.dma_start(raw_a[:, s, 0:whole, :], src.rearrange("a p k r -> (a p) k r")).then_inc(ad_in, 16)
                    if tail:
                        src = ad_last[bass.ds(slot1[s], 1)].rearrange("a p r -> (a p) r")
                        sp.dma_start(raw_a[0:F_LAST, s, whole, :], src).then_inc(ad_in, 16)

            def load_down_w(b, ht, tiles):
                whole = tiles - 1 if isinstance(b, int) else tiles
                sp.wait_ge(d_ok, b * KT + (ht + 1))
                src = wdT[bass.ds(b * (BLOCK * P), whole * P), ht * P:(ht + 1) * P]
                sp.dma_start(raw_d[:, ht % 2, 0:whole, :],
                             src.rearrange("(k p) f -> p k f", p=P)).then_inc(d_in[ht % 2], 16)
                if whole < tiles:
                    sp.dma_start(raw_d[0:F_LAST, ht % 2, whole, :],
                                 wdT[F - F_LAST:F, ht * P:(ht + 1) * P]).then_inc(d_in[ht % 2], 16)

            load_f_w(0, 0)
            sp.wait_ge(bgu_gathered, 16 * SEQS)
            load_f_b(0, 0)
            load_f_w(0, 1)
            load_f_b(0, 1)
            for s in range(SEQS):
                sp.dma_start(bd_rows[s * RANK:(s + 1) * RANK, :],
                             bd[bass.ds(slot1[s], 1)].rearrange("a r f -> (a r) f")).then_inc(bd_gathered, 16)
            with sp.Fori(0, BLOCKS) as b:
                load_f_w(b, 2)
                load_f_b(b, 2)
                load_f_w(b, 3)
                load_f_b(b, 3)
                load_down_a(b, BLOCK)
                load_down_w(b, 0, BLOCK)
                load_down_w(b, 1, BLOCK)
                load_f_w(b, 4)
                load_f_b(b, 4)
                load_down_w(b, 2, BLOCK)
                load_down_w(b, 3, BLOCK)
                load_f_w(b, 5)
                load_f_b(b, 5)
            load_f_w(BLOCKS, 2, F_LAST)
            load_last_f_b(FT - 1)
            load_down_a(BLOCKS, TAIL)
            for ht in range(2):
                load_down_w(BLOCKS, ht, TAIL)
            sp.wait_ge(bd_gathered, 16 * SEQS)
            for o in range(KT // 2):
                sp.wait_ge(b_ok, STAGE_BD + o - 1)
                load_b((STAGE_BD + o) % 2, bd_rows, o * BW, BW, b_in[(STAGE_BD + o) % 2])
                load_down_w(BLOCKS, 2 + o, TAIL)
            for i, (out, ht, h, part) in enumerate(out_parts):
                sp.wait_ge(added, CREDIT + BLOCKS * 2 * KT + i + 1)
                sp.dma_start(outT[ht, :, of_half(h, part)], x[:, ht, of_half(h, part)]).then_inc(out_done, 16)
            sp.wait_ge(out_done, 16 * len(out_parts))

        @block.scalar
        def _(eng):
            eng.sem_inc(silu_ok, CREDIT)
            eng.dma_start(x[:, 0, cols(0)], xT[0, :, 0]).then_inc(x_in[0], 16)
            eng.wait_ge(zeros_ok, 1)
            eng.activation(act[0:1, 0, 0:2], f32(zeros[0:1, 0:2]), ACT.Silu)

            def round_to(out, in_, scale=1.0):
                return eng.activation(out, in_, ACT.Copy, scale=scale)

            def x_hi(h, k):
                eng.wait_ge(x_in_late if h else x_in[k], 16)
                round_to(act_hi[:, k, cols(h)], x[:, k, cols(h)]).then_inc(x_hi_ok, 1)

            def b_hi_part(slot):
                round_to(b_x[:, slot], raw_b[:, slot], cst[:, C_SB:C_SB + 1]).then_inc(b_hi_ok, 1)

            def a_hi_part():
                for h in range(2):
                    last = round_to(a_part(h, 0), a_whole(h))
                last.then_inc(a_hi_ok, 1)

            def t_low_part(n, h):
                eng.wait_ge(t_psum_ok, n)
                for a in range(2):
                    last = round_to(t_low[32 * a:32 * a + 32, h, :],
                                    t_bank[h][64 + 32 * a:96 + 32 * a, a * PAIR:(a + 1) * PAIR])
                last.then_inc(t_low_ok, 1)

            def t_hi_part(n, h, places, rows):
                eng.wait_ge(t_whole_ok, n)
                round_to(t_hi[0:rows, h, :], t_whole[0:rows, h, :]).then_inc(t_round_ok, 1)
                for out, src in places(h, 0):
                    last = round_to(out, t_whole[src, h, :])
                last.then_inc(t_hi_ok, 1)

            def x1_hi_part(h, ot):
                eng.wait_ge(x1_ok, h * KT + ot + 1)
                round_to(x1_hi[:, ot, cols(h)], x[:, ot, cols(h)]).then_inc(x1_hi_ok, 1)

            eng.wait_ge(w_in[0][0], 16)
            round_to(w_hi[:, 0, 0], raw_w[:, 0, 0]).then_inc(w0_hi_ok, 1)
            for k in range(KT):
                x_hi(0, k)
            eng.wait_ge(w_in[0][1], 16)
            round_to(w_hi[:, 0, 1], raw_w[:, 0, 1]).then_inc(w_hi_ok, 1)
            eng.wait_ge(w_in[1][0], 16)
            eng.wait_ge(w_in[1][1], 16)
            round_to(w_hi[:, 1], raw_w[:, 1]).then_inc(w_hi_ok, 1)
            for k in range(KT):
                x_hi(1, k)
            eng.wait_ge(a0_in, 16 * SEQS)
            a_hi_part()
            for h in range(2):
                t_low_part(h + 1, h)
            for h in range(2):
                t_hi_part(h + 1, h, t_pairs, 64)
            eng.wait_ge(cst_in, 16)
            eng.wait_ge(b0_in, 16 * 3)
            for s in range(2):
                b_hi_part(s)
            eng.wait_ge(agu_in, 16 * SEQS)
            eng.wait_ge(w_free, 1)
            for s in range(SEQS):
                dst, src = agu_views(w_hi, s)
                last = round_to(dst, src)
            last.then_inc(agu_hi_ok, 1)

            def w_f_hi(b, j):
                for o in range(2):
                    eng.wait_ge(w_in[w_slot(j)][o], f_in_count(b, j))
                if j == 1:
                    eng.wait_ge(t_psum_ok, 4)
                else:
                    eng.wait_ge(w_free, b * BLOCK + (STAGE_A + max(j - 1, 0)))
                round_to(w_hi[:, w_slot(j)], raw_w[:, w_slot(j)]).then_inc(f_hi_ok, 1)

            def b_f_hi(b, j, more=0):
                eng.wait_ge(b_in[b_slot(j)], b_in_count(b, j) + more)
                if j >= 2:
                    eng.wait_ge(up_ok, b * (2 * BLOCK) + 2 * j)
                b_hi_part(b_slot(j))

            def f_hi(b, j, more=0):
                w_f_hi(b, j)
                b_f_hi(b, j, more)

            def a_d_hi(b, landed):
                eng.wait_ge(ad_in, landed)
                eng.wait_ge(a_free, b + 1)
                a_hi_part()

            def d_hi_part(b, ht, landed):
                eng.wait_ge(d_in[ht % 2], landed)
                if ht >= 2 and isinstance(b, int):
                    eng.wait_ge(d_free, ht - 1)
                elif ht >= 2:
                    eng.wait_ge(down_ok, b * (2 * KT) + (2 * ht - 2))
                round_to(wd_hi[:, ht % 2], raw_d[:, ht % 2]).then_inc(d_hi_ok, 1)

            def gate_tile(b, j, rows):
                for h in range(2):
                    n = 2 * (b * BLOCK + j) + h
                    eng.wait_ge(gate_ok, n + 1)
                    eng.wait_ge(act_ok, n + 1)
                    eng.activation(sil[0:rows, h], gu_bank[h][0][0:rows], ACT.Silu).then_inc(silu_ok, 1)
                    eng.wait_ge(act_ok, CREDIT + n + 1)
                    round_to(act_hi[0:rows, j, cols(h)], act[0:rows, h]).then_inc(act_hi_ok, 1)

            for ot in range(KT):
                x1_hi_part(0, ot)
            w_f_hi(0, 0)
            for ot in range(KT):
                x1_hi_part(1, ot)
            b_f_hi(0, 0)
            for h in range(2):
                t_hi_part(3 + h, h, tgu_pairs, P)
                if h == 0:
                    f_hi(0, 1)

            with eng.Fori(0, BLOCKS) as b:
                gate_tile(b, 0, P)
                f_hi(b, 2)
                gate_tile(b, 1, P)
                f_hi(b, 3)
                a_d_hi(b, 16 * SEQS * (b + 1))
                gate_tile(b, 2, P)
                f_hi(b, 4)
                for ht in range(2):
                    d_hi_part(b, ht, 32 * b + 16)
                gate_tile(b, 3, P)
                f_hi(b, 5)
                for ht in range(2, KT):
                    d_hi_part(b, ht, 32 * b + 32)
            extra = [64 if (STAGE_BD + o) % 2 == b_slot(TAIL - 1) else 0 for o in range(2)]
            gate_tile(BLOCKS, 0, P)
            f_hi(BLOCKS, 2, 64)
            a_d_hi(BLOCKS, 16 * SEQS * (BLOCKS + 2))
            d_hi_part(BLOCKS, 0, 32 * BLOCKS + 32)
            gate_tile(BLOCKS, 1, P)
            d_hi_part(BLOCKS, 1, 32 * BLOCKS + 32)
            b_f_hi(BLOCKS, TAIL, extra[0])
            gate_tile(BLOCKS, 2, F_LAST)
            b_f_hi(BLOCKS, TAIL + 1, extra[1])
            for h in range(2):
                t_low_part(5 + h, h)
                if h == 1:
                    d_hi_part(BLOCKS, 2, 32 * BLOCKS + 64)
                t_hi_part(5 + h, h, t_pairs, 64)
            d_hi_part(BLOCKS, 3, 32 * BLOCKS + 64)

        @block.vector
        def _(eng):
            eng.sem_inc(act_ok, CREDIT)
            eng.sem_inc(d_ok, CREDIT)
            eng.sem_inc(added, CREDIT)

            def minus(out, whole, hi):
                return eng.tensor_tensor(out, whole, f32(hi), ALU.subtract)

            def x_lo_part(h, k):
                eng.wait_ge(x_hi_ok, h * KT + k + 1)
                minus(act_lo[:, k, cols(h)], x[:, k, cols(h)], act_hi[:, k, cols(h)]).then_inc(x_lo_dve, 1)

            def b_lo_part(n, slot):
                eng.wait_ge(b_hi_ok, n)
                eng.scalar_tensor_tensor(out=b_x[:, slot].rearrange("p a o f -> p (a o f)"),
                                         in0=raw_b[:, slot].rearrange("p a o f -> p (a o f)"),
                                         scalar=cst[:, C_LB:C_LB + 1],
                                         in1=f32(b_x[:, slot].rearrange("p a o f -> p (a o f)")),
                                         op0=ALU.mult, op1=ALU.add).then_inc(b_ok, 1)

            def a_lo_part(n):
                eng.wait_ge(a_hi_ok, n)
                for h in range(2):
                    last = minus(a_part(h, 1), a_whole(h), a_part(h, 0))
                last.then_inc(a_ok, 1)

            def t_summed(h, mask, sums):
                eng.wait_ge(t_low_ok, sums // 2)
                for a in range(2):
                    row, col = slice(32 * a, 32 * a + 32), slice(a * PAIR, (a + 1) * PAIR)
                    eng.tensor_tensor(t_sum[row, h, :], t_bank[h][row, col], t_low[row, h, :],
                                      ALU.add).then_inc(t_sum_ok, 1)
                eng.wait_ge(t_sum_ok, sums)
                eng.tensor_tensor(t_whole[0:64, h, :], t_sum[:, h, :], cst[0:64, mask:mask + PAIR],
                                  ALU.mult).then_inc(t_whole_ok, 1)

            def t_gate_up(n, h):
                eng.wait_ge(t_psum_ok, n)
                for a in range(2):
                    row, col = slice(64 * a, 64 * a + 64), slice(a * PAIR, (a + 1) * PAIR)
                    last = eng.tensor_tensor(t_whole[row, h, :], d_bank[h][row, col],
                                             cst[row, C_MASK1:C_MASK1 + PAIR], ALU.mult)
                last.then_inc(t_whole_ok, 1)

            def t_lo_part(n, h, places):
                eng.wait_ge(t_round_ok, n)
                for out, src in places(h, 2):
                    last = minus(out, t_whole[src, h, :], t_hi[src, h, :])
                last.then_inc(t_lo_ok, 1)

            def x1_part(h, ot):
                eng.wait_ge(l0_ok, h * KT + ot + 1)
                eng.scalar_tensor_tensor(out=x[:, ot, cols(h)], in0=l0_bank[h * KT + ot][:, :],
                                         scalar=bias_sb[:, ot:ot + 1], in1=x[:, ot, cols(h)],
                                         op0=ALU.add, op1=ALU.add).then_inc(x1_ok, 1)

            eng.wait_ge(w0_hi_ok, 1)
            minus(w_lo[:, 0, 0], raw_w[:, 0, 0], w_hi[:, 0, 0]).then_inc(w0_ok, 1)
            for k in range(KT):
                x_lo_part(0, k)
            eng.wait_ge(w_hi_ok, 1)
            minus(w_lo[:, 0, 1], raw_w[:, 0, 1], w_hi[:, 0, 1]).then_inc(w_ok, 1)
            eng.wait_ge(w_hi_ok, 2)
            minus(w_lo[:, 1], raw_w[:, 1], w_hi[:, 1]).then_inc(w_ok, 1)
            x_lo_part(1, 1)
            x_lo_part(1, 3)
            a_lo_part(1)
            eng.wait_ge(cst_in, 16)
            for h in range(2):
                t_summed(h, C_MASK0, 2 * h + 2)
            for h in range(2):
                t_lo_part(h + 1, h, t_pairs)
            b_lo_part(1, 0)
            b_lo_part(2, 1)

            def x1_lo(h, ot):
                eng.wait_ge(x1_hi_ok, h * KT + ot + 1)
                minus(x1_lo_sb[:, ot, cols(h)], x[:, ot, cols(h)], x1_hi[:, ot, cols(h)]).then_inc(x1_lo_dve, 1)

            eng.wait_ge(bias_in, 16)
            for h in range(2):
                x1_part(h, 0)
                if h == 1:
                    x1_lo(0, 3)
                x1_part(h, 1)
                x1_part(h, 2)
                x1_lo(h, 1)
                x1_part(h, 3)
                x1_lo(h, 2)
            x1_lo(1, 3)

            def b_f_lo(b, j):
                b_lo_part(b * BLOCK + (STAGE_BF + j + 1), b_slot(j))

            def d_lo_part(b, ht):
                eng.wait_ge(d_hi_ok, b * KT + (ht + 1))
                minus(wd_lo[:, ht % 2], raw_d[:, ht % 2], wd_hi[:, ht % 2]).then_inc(d_ok, 1)

            def up_tile(b, j, rows):
                for h in range(2):
                    n = 2 * (b * BLOCK + j) + h
                    eng.wait_ge(up_ok, CREDIT + n + 1)
                    eng.wait_ge(silu_ok, CREDIT + n + 1)
                    eng.wait_ge(act_lo_ok, n + 1)
                    eng.tensor_tensor(act[0:rows, h], gu_bank[h][1][0:rows], sil[0:rows, h],
                                      ALU.mult).then_inc(act_ok, 1)

            def add_down(b, ht, banks):
                for h in range(2):
                    eng.wait_ge(down_ok, b * (2 * KT) + (2 * ht + h + 1))
                    eng.tensor_tensor(x[:, ht, cols(h)], banks[h][:, :], x[:, ht, cols(h)],
                                      ALU.add).then_inc(added, 1)

            b_f_lo(0, 0)
            for h in range(2):
                t_gate_up(3 + h, h)
                t_lo_part(3 + h, h, tgu_pairs)
            b_f_lo(0, 1)

            with eng.Fori(0, BLOCKS) as b:
                up_tile(b, 0, P)
                b_f_lo(b, 2)
                up_tile(b, 1, P)
                b_f_lo(b, 3)
                a_lo_part(b + 2)
                up_tile(b, 2, P)
                b_f_lo(b, 4)
                d_lo_part(b, 0)
                d_lo_part(b, 1)
                up_tile(b, 3, P)
                b_f_lo(b, 5)
                for ht in range(KT):
                    add_down(b, ht, d_bank)
                    if ht + 2 < KT:
                        d_lo_part(b, ht + 2)
            up_tile(BLOCKS, 0, P)
            b_f_lo(BLOCKS, 2)
            a_lo_part(BLOCKS + 2)
            d_lo_part(BLOCKS, 0)
            up_tile(BLOCKS, 1, P)
            d_lo_part(BLOCKS, 1)
            b_f_lo(BLOCKS, TAIL)
            up_tile(BLOCKS, 2, F_LAST)
            for h in range(2):
                t_summed(h, C_MASK1, 2 * h + 6)
                t_lo_part(5 + h, h, t_pairs)
            b_f_lo(BLOCKS, TAIL + 1)
            for i, (out, ht, h, part) in enumerate(out_parts):
                eng.wait_ge(down_ok, BLOCKS * (2 * KT) + i + 1)
                eng.tensor_tensor(x[:, ht, of_half(h, part)], out[:, part],
                                  x[:, ht, of_half(h, part)], ALU.add).then_inc(added, 1)

        @block.gpsimd
        def _(eng):
            eng.sem_inc(act_lo_ok, CREDIT)
            eng.memset(f32(zeros[:, :]), 0.0).then_inc(zeros_ok, 1)

            def minus(out, whole, hi):
                return eng.tensor_tensor(out, whole, f32(hi), ALU.subtract)

            eng.dma_start(idx[:, :], indices).then_inc(idx_in, 16)
            eng.wait_ge(idx_in, 16)
            slot1 = slots(mybir.EngineType.Pool, SEQS, SLOTS1)
            for s in range(SEQS):
                eng.dma_start(raw_agu[:, s, :, :, :], agu[bass.ds(slot1[s], 1)].rearrange(
                    "a p o k r -> (a p) o k r")).then_inc(agu_in, 16)
            for k in (0, 2):
                eng.wait_ge(x_hi_ok, KT + k + 1)
                minus(act_lo[:, k, cols(1)], x[:, k, cols(1)], act_hi[:, k, cols(1)]).then_inc(x_lo_pool, 1)
            eng.wait_ge(agu_hi_ok, 1)
            for s in range(SEQS):
                hi, src = agu_views(w_hi, s)
                dst, _ = agu_views(w_lo, s)
                last = minus(dst, src, hi)
            last.then_inc(agu_ok, 1)
            for h in range(2):
                eng.wait_ge(x1_hi_ok, h * KT + 1)
                minus(x1_lo_sb[:, 0, cols(h)], x[:, 0, cols(h)], x1_hi[:, 0, cols(h)]).then_inc(x1_lo_pool, 1)

            def f_lo(b, j):
                eng.wait_ge(f_hi_ok, b * BLOCK + (j + 1))
                minus(w_lo[:, w_slot(j)], raw_w[:, w_slot(j)], w_hi[:, w_slot(j)]).then_inc(f_ok, 1)

            def act_lo_tile(b, j, rows):
                for h in range(2):
                    eng.wait_ge(act_hi_ok, 2 * (b * BLOCK + j) + h + 1)
                    minus(act_lo[0:rows, j, cols(h)], act[0:rows, h],
                          act_hi[0:rows, j, cols(h)]).then_inc(act_lo_ok, 1)

            f_lo(0, 0)
            f_lo(0, 1)
            with eng.Fori(0, BLOCKS) as b:
                for j in range(BLOCK):
                    act_lo_tile(b, j, P)
                    f_lo(b, j + 2)
            act_lo_tile(BLOCKS, 0, P)
            f_lo(BLOCKS, 2)
            act_lo_tile(BLOCKS, 1, P)
            act_lo_tile(BLOCKS, 2, F_LAST)
            for ht in range(2, KT):
                eng.wait_ge(d_hi_ok, BLOCKS * KT + ht + 1)
                minus(wd_lo[:, ht % 2], raw_d[:, ht % 2], wd_hi[:, ht % 2]).then_inc(d_ok, 1)

        @block.tensor
        def _(eng):
            eng.sem_inc(up_ok, CREDIT)

            def split_product(out, hi, lo, in_hi, in_lo, start, stop=False):
                eng.matmul(out, hi, in_hi, start=start, stop=False)
                eng.matmul(out, hi, in_lo, start=False, stop=False)
                return eng.matmul(out, lo, in_hi, start=False, stop=stop)

            def wide_sum(out, slot, o, in_hi, in_lo, h, ks=range(KT)):
                for k in ks:
                    last = split_product(out, w_hi[:, slot, o, k, :], w_lo[:, slot, o, k, :],
                                         in_hi[:, k, cols(h)], in_lo[:, k, cols(h)], k == 0)
                return last

            def lora(out, slot, o, t, h):
                for a in range(2):
                    last = eng.matmul(out[:, a * PAIR:(a + 1) * PAIR], b_x[:, slot, 2 * h + a, o, :],
                                      t[:, 2 * h + a, :], start=False, stop=a == 1)
                return last

            def l0_main(h, ot):
                return wide_sum(l0_bank[h * KT + ot][:, :], ot // 2, ot % 2, act_hi, act_lo, h)

            def project(out, h, n_k, start, first, k_rows=P, stop=True):
                for k in range(n_k):
                    if first is not None:
                        eng.wait_ge(act_lo_ok, first + 2 * k)
                    rows = slice(0, k_rows if k == n_k - 1 else P)
                    for v in (act_hi, act_lo):
                        last = eng.matmul(out, a_x[rows, k, h, :, :].rearrange("p v c -> p (v c)"),
                                          v[rows, k, cols(h)], start=start and k == 0 and v is act_hi,
                                          stop=stop and k == n_k - 1 and v is act_lo)
                return last

            def t_ready(n):
                eng.wait_ge(t_hi_ok, n)
                eng.wait_ge(t_lo_ok, n)

            def l0_lora(h, ot):
                return lora(l0_bank[h * KT + ot], ot // 2, ot % 2, t_x, h).then_inc(l0_ok, 1)

            eng.wait_ge(zeros_ok, 1)
            for _ in range(WARM_UP):
                eng.matmul(d_bank[0][:, :], zeros[:, 0:P], zeros[:, :], start=True, stop=True)
            eng.wait_ge(w0_hi_ok, 1)
            for k in range(KT):
                w, v, out = w_hi[:, 0, 0, k, :], act_hi[:, k, cols(0)], l0_bank[0][:, :]
                eng.wait_ge(x_hi_ok, k + 1)
                eng.matmul(out, w, v, start=k == 0, stop=False)
                if k == 0:
                    eng.wait_ge(w0_ok, 1)
                eng.matmul(out, w_lo[:, 0, 0, k, :], v, start=False, stop=False)
                eng.wait_ge(x_lo_dve, k + 1)
                eng.matmul(out, w, act_lo[:, k, cols(0)], start=False, stop=False)
            eng.wait_ge(w_ok, 1)
            l0_main(0, 1)
            eng.wait_ge(w_ok, 2)
            l0_main(0, 2)
            l0_main(0, 3)
            eng.wait_ge(a_ok, 1)
            project(t_bank[0][:, :], 0, KT, True, None).then_inc(t_psum_ok, 1)
            eng.wait_ge(x_lo_pool, 2)
            eng.wait_ge(x_lo_dve, KT + 2)
            project(t_bank[1][:, :], 1, KT, True, None).then_inc(t_psum_ok, 1)
            eng.sem_inc(a_free, 1)
            l0_main(1, 0)
            l0_main(1, 1).then_inc(w_free, 1)
            t_ready(1)
            wide_sum(l0_bank[KT + 2][:, :], 1, 0, act_hi, act_lo, 1, ks=(0, 1))
            for s in range(2):
                eng.wait_ge(b_ok, s + 1)
                for ot in (2 * s, 2 * s + 1):
                    l0_lora(0, ot)
                wide_sum(l0_bank[KT + 2][:, :], 1, 0, act_hi, act_lo, 1, ks=(2 + s,))
            t_ready(2)
            for ot in range(KT - 1):
                l0_lora(1, ot)
            l0_main(1, 3).then_inc(w_free, 1)
            l0_lora(1, KT - 1)

            for h in range(2):
                eng.wait_ge(x1_ok, KT + h + 1)
                if h == 0:
                    eng.wait_ge(agu_ok, 1)
                for k in range(KT):
                    if k == 0:
                        eng.wait_ge(x1_lo_pool, h + 1)
                    else:
                        eng.wait_ge(x1_lo_dve, h * (KT - 1) + k)
                    last = split_product(d_bank[h][:, :], w_hi[:, STAGE_A % 2, h, k, :],
                                         w_lo[:, STAGE_A % 2, h, k, :], x1_hi[:, k, cols(h)],
                                         x1_lo_sb[:, k, cols(h)], k == 0, k == KT - 1)
                last.then_inc(t_psum_ok, 1)
            for h in range(2):
                eng.matmul(t_bank[h][:, :], zeros[:, 0:P], zeros[:, :], start=True, stop=False)

            def f_tile(b, j, last_tile=False):
                width = F_LAST if last_tile else P
                t = b * BLOCK + j
                ws, bs = w_slot(j), b_slot(j)
                eng.wait_ge(f_ok, t + 1)
                for h in range(2):
                    n = 2 * t + h
                    for o in range(2):
                        eng.wait_ge((silu_ok, act_ok)[o], n + 1)
                        for k in range(KT):
                            last = split_product(gu_bank[h][o][0:width, :], w_hi[:, ws, o, k, 0:width],
                                                 w_lo[:, ws, o, k, 0:width], x1_hi[:, k, cols(h)],
                                                 x1_lo_sb[:, k, cols(h)], k == 0)
                    if h == 1:
                        last.then_inc(w_free, 1)
                    else:
                        eng.wait_ge(b_ok, t + (STAGE_BF + 1))
                    t_ready(3 + h)
                    for o in range(2):
                        for a in range(2):
                            last = eng.matmul(gu_bank[h][o][0:width, a * PAIR:(a + 1) * PAIR],
                                              b_x[:, bs, 2 * h + a, o, 0:width], tgu_x[:, 2 * h + a, o, :],
                                              start=False, stop=a == 1)
                        last.then_inc((gate_ok, up_ok)[o], 1)

            def down_sum(out, ht, h, n_k, k_rows=P, stop=True, part=slice(0, HALF)):
                for k in range(n_k):
                    rows = slice(0, k_rows if k == n_k - 1 else P)
                    last = split_product(out[:, part], wd_hi[rows, ht % 2, k, :], wd_lo[rows, ht % 2, k, :],
                                         act_hi[rows, k, of_half(h, part)], act_lo[rows, k, of_half(h, part)],
                                         k == 0, stop and k == n_k - 1)
                return last

            with eng.Fori(0, BLOCKS) as b:
                for j in range(BLOCK):
                    f_tile(b, j)
                eng.wait_ge(a_ok, b + 2)
                for n in range(2 * KT):
                    ht, h = n // 2, n % 2
                    if ht == 0:
                        last = project(t_bank[h][:, :], h, BLOCK, False, b * (2 * BLOCK) + (CREDIT + h + 1),
                                       stop=False)
                        if h == 1:
                            last.then_inc(a_free, 1)
                    if h == 0:
                        eng.wait_ge(d_ok, b * KT + (CREDIT + ht + 1))
                    eng.wait_ge(added, b * (2 * KT) + (n + 1))
                    down_sum(d_bank[h][:, :], ht, h, BLOCK).then_inc(down_ok, 1)
            for j in range(TAIL):
                f_tile(BLOCKS, j, j == TAIL - 1)

            eng.wait_ge(a_ok, BLOCKS + 2)

            def down_main(n):
                ht, h = n // 2, n % 2
                eng.wait_ge(d_ok, BLOCKS * KT + CREDIT + ht + 1)
                if n < 2:
                    project(t_bank[h][:, :], h, TAIL, False, BLOCKS * 2 * BLOCK + CREDIT + h + 1,
                            F_LAST).then_inc(t_psum_ok, 1)
                    eng.wait_ge(added, BLOCKS * 2 * KT + n + 1)
                elif n >= 6:
                    eng.wait_ge(added, BLOCKS * 2 * KT + CREDIT + n - 5)
                last = down_sum(tail_bank[n][:, :], ht, h, TAIL, F_LAST, stop=False)
                if h == 1:
                    last.then_inc(d_free, 1)

            def down_lora(n):
                ht, h = n // 2, n % 2
                if n < 2:
                    t_ready(5 + n)
                eng.wait_ge(b_ok, STAGE_BD + ht // 2 + 1)
                lora(tail_bank[n], (STAGE_BD + ht // 2) % 2, ht % 2, t_x, h).then_inc(down_ok, 1)

            for n, loras in enumerate([(), (), (0,), (1, 2), (3,), (4, 5), (6,)]):
                down_main(n)
                for m in loras:
                    down_lora(m)
            eng.wait_ge(added, BLOCKS * 2 * KT + CREDIT + 3)
            for a, (out, ht, h, part) in enumerate(out_parts[-2:]):
                down_sum(out, ht, h, TAIL, F_LAST, stop=False, part=part)
                eng.matmul(out[:, part], b_x[:, (STAGE_BD + ht // 2) % 2, 2 * h + a, ht % 2, :],
                           t_x[:, 2 * h + a, :], start=False, stop=True).then_inc(down_ok, 1)


def kernel(x, itok_B_0_23, itok_B_2_6, L0_cond_W, L0_cond_b, L0_cond_lora_As, L0_cond_lora_Bs, L1_cond_W_gate,
           L1_cond_W_up, L1_cond_W_down, L1_cond_A_gate, L1_cond_B_gate, L1_cond_A_up, L1_cond_B_up,
           L1_cond_A_down, L1_cond_B_down):
    import numpy as np
    import concourse.bacc as bacc
    from concourse.bass_utils import run_bass_kernel_spmd

    def tiles(a):
        return a.reshape(a.shape[0], -1, P, a.shape[-1]).transpose(0, 2, 1, 3)

    p, t = np.arange(P), np.arange(PAIR)
    same = (p[:, None] % 32 // RANK == t[None, :] // SEQ_LEN).astype(np.float32)
    b_low = (p // 32 % 2).astype(np.float32)
    consts = np.concatenate([same * 2.0, same * 0.5, np.stack([1 - 2 * b_low, b_low], 1)],
                            axis=1).astype(np.float32)

    whole = (FT - 1) * P
    b_gate, b_up = (a[0].transpose(0, 2, 1) for a in (L1_cond_B_gate, L1_cond_B_up))
    b_gu = np.stack([b_gate[:, :, :whole].reshape(SLOTS1, RANK, FT - 1, P),
                     b_up[:, :, :whole].reshape(SLOTS1, RANK, FT - 1, P)], axis=3)
    b_last = np.stack([b_gate[:, :, whole:], b_up[:, :, whole:]], axis=2)
    arrays = {
        "xT": x.reshape(2, HALF, KT, P).transpose(0, 3, 2, 1),
        "indices": np.concatenate([itok_B_0_23, itok_B_2_6]).reshape(1, 2 * SEQS),
        "w0T": L0_cond_W.reshape(KT, P, KT, P).transpose(0, 3, 2, 1),
        "bias": L0_cond_b.reshape(KT, P).T,
        "a0": tiles(L0_cond_lora_As),
        "b0": L0_cond_lora_Bs,
        "wgT": L1_cond_W_gate.T,
        "wuT": L1_cond_W_up.T,
        "agu": np.stack([tiles(a[0].transpose(0, 2, 1)) for a in (L1_cond_A_gate, L1_cond_A_up)], axis=2),
        "bgu": np.concatenate([b_gu.reshape(SLOTS1, RANK, -1),
                               b_last.reshape(SLOTS1, RANK, -1)], axis=2),
        "wdT": L1_cond_W_down.T,
        "ad": tiles(L1_cond_A_down[0].transpose(0, 2, 1)[:, :whole]),
        "ad_last": L1_cond_A_down[0].transpose(0, 2, 1)[:, whole:],
        "bd": L1_cond_B_down[0].transpose(0, 2, 1),
        "consts": consts,
    }
    arrays = {name: np.ascontiguousarray(a) for name, a in arrays.items()}
    nc = bacc.Bacc("TRN2", target_bir_lowering=False, num_devices=1)
    ins = {name: nc.dram_tensor(name, a.shape, mybir.dt.from_np(a.dtype), kind="ExternalInput").ap()
           for name, a in arrays.items()}
    outT = nc.dram_tensor("outT", (KT, P, TOKENS), F32, kind="ExternalOutput").ap()
    build(nc, outT=outT, **ins)
    result = run_bass_kernel_spmd(nc, [arrays], core_ids=[0])
    return result.results[0]["outT"].reshape(H, TOKENS).T.reshape(SEQS, SEQ_LEN, H)
```
